# Optimizing a Trainium2 kernel written in Bass

```python
import numpy as np
import jax
import jax.numpy as jnp

def _softmax(x, axis=-1):
    return jax.nn.softmax(x, axis=axis)

def _gelu(x):
    return jax.nn.gelu(x, approximate=True)

def _silu(x):
    return jax.nn.silu(x)

def _sigmoid(x):
    return jax.nn.sigmoid(x)

def _layernorm(x, axis=-1, eps=1e-05):
    m = jnp.mean(x, axis=axis, keepdims=True)
    v = jnp.var(x, axis=axis, keepdims=True)
    return (x - m) / jnp.sqrt(v + eps)

def _scatter_add(tgt, idx, src, axis=0):
    return tgt.at[idx].add(src)

def _segment_sum(src, seg, n):
    return jax.ops.segment_sum(src, seg, n)
kernel_name = 'mk_lm_tower_d1_tok_ids768_r4_089d93'

def setup_inputs(seed: int=0):
    np.random.seed(seed)
    _w = jnp.asarray

    def _rec_inputs():
        import jax
        import jax.numpy as jnp
        _rk = jax.random.key(seed)
        x = jax.random.randint(jax.random.fold_in(_rk, 1), (2, 2048), 0, 12564, jnp.int32)
        return x
    x = _rec_inputs()

    def _L0_tok_setup():
        import jax, jax.numpy as jnp
        import numpy as np
        NF4_LEVELS = jnp.array([-1.0, -0.6961928009986877, -0.5250730514526367, -0.39491748809814453, -0.28444138169288635, -0.18477343022823334, -0.09105003625154495, 0.0, 0.07958029955625534, 0.16093020141124725, 0.24611230194568634, 0.33791524171829224, 0.44070982933044434, 0.5626170039176941, 0.8481764793395996, 1.0], dtype=jnp.float32)
        NF4_MIDPOINTS = (NF4_LEVELS[1:] + NF4_LEVELS[:-1]) * 0.5
        BLOCK_SIZE = 64
        SIGMA_FACTOR = 3.0
        EPS = 1e-12

        def fake_quantize_tcfp12(x, block_size=BLOCK_SIZE, nf4_residual=True, nf_aware_scaling=True, sigma_factor=SIGMA_FACTOR):
            shape = x.shape
            xb = x.reshape(-1, block_size)
            absmax = jnp.max(jnp.abs(xb), axis=1, keepdims=True)
            if nf_aware_scaling:
                std = jnp.std(xb, axis=1, keepdims=True)
                scale = jnp.minimum(absmax, sigma_factor * std)
            else:
                scale = absmax
            scale = jnp.maximum(scale, EPS)
            q = jnp.clip(jnp.round(xb / scale * 127.0), -127.0, 127.0)
            main = q * (scale / 127.0)
            res = xb - main
            if nf4_residual:
                rmax = jnp.maximum(jnp.max(jnp.abs(res), axis=1, keepdims=True), EPS)
                rn = res / rmax
                idx = jnp.searchsorted(NF4_MIDPOINTS, rn)
                rq = NF4_LEVELS[idx] * rmax
            else:
                rmax = jnp.maximum(jnp.max(jnp.abs(res), axis=1, keepdims=True), EPS)
                rq = jnp.clip(jnp.round(res / rmax * 7.0), -7.0, 7.0) * (rmax / 7.0)
            return (main + rq).reshape(shape)

        def ste_fake_quantize(x):
            return x + jax.lax.stop_gradient(fake_quantize_tcfp12(x) - x)
        key = jax.random.key(seed)
        k1, k2 = jax.random.split(key)
        num_embeddings, embedding_dim = (50257, 192)
        batch, seq = (8, 1024)
        indices = jax.random.randint(k1, (batch, seq), 0, num_embeddings, dtype=jnp.int64 if jax.config.jax_enable_x64 else jnp.int32)
        weight = jax.random.normal(k2, (num_embeddings, embedding_dim), dtype=jnp.float32)
        weight = weight.at[0].set(0.0)
        return {'indices': indices, 'weight': weight}
    _L0_tok_all = _L0_tok_setup()
    _L0_tok_in = {k: v for k, v in _L0_tok_all.items() if k in ('weight',)}
    del _L0_tok_all

    def _L0_attn_setup():
        import jax, jax.numpy as jnp
        import numpy as np
        import math
        D_MODEL, N_HEADS, D_HEAD, SEQ, BATCH = (192, 12, 64, 256, 8)
        INIT_RANGE = 0.02
        key = jax.random.key(seed)
        ks = jax.random.split(key, 6)
        x = jax.random.normal(ks[0], (BATCH, SEQ, D_MODEL), dtype=jnp.float32)
        W_Q = jax.random.normal(ks[1], (N_HEADS, D_MODEL, D_HEAD), dtype=jnp.float32) * INIT_RANGE
        W_K = jax.random.normal(ks[2], (N_HEADS, D_MODEL, D_HEAD), dtype=jnp.float32) * INIT_RANGE
        W_V = jax.random.normal(ks[3], (N_HEADS, D_MODEL, D_HEAD), dtype=jnp.float32) * INIT_RANGE
        W_O = jax.random.normal(ks[4], (N_HEADS, D_HEAD, D_MODEL), dtype=jnp.float32) * INIT_RANGE
        b_Q = jnp.zeros((N_HEADS, D_HEAD), dtype=jnp.float32)
        b_K = jnp.zeros((N_HEADS, D_HEAD), dtype=jnp.float32)
        b_V = jnp.zeros((N_HEADS, D_HEAD), dtype=jnp.float32)
        b_O = jnp.zeros((D_MODEL,), dtype=jnp.float32)
        return {'normalized_resid_pre': x, 'W_Q': W_Q, 'b_Q': b_Q, 'W_K': W_K, 'b_K': b_K, 'W_V': W_V, 'b_V': b_V, 'W_O': W_O, 'b_O': b_O}
    _L0_attn_all = _L0_attn_setup()
    _L0_attn_in = {k: v for k, v in _L0_attn_all.items() if k in ('W_Q', 'b_Q', 'W_K', 'b_K', 'W_V', 'b_V', 'W_O', 'b_O')}
    del _L0_attn_all

    def _L0_ffn_setup():
        import jax, jax.numpy as jnp
        import numpy as np
        B, T, D = (2, 512, 192)
        S, R, M, K = (8, 16, 64, 4)
        H, G = (32, 64)

        def _ssinf3(x, P, C, W1, b1, W2, b2, G1, g1b, G2, g2b):
            shp = x.shape
            xf = x.reshape(-1, shp[-1])
            z = jnp.einsum('nd,sdr->nsr', xf, P)
            scores = jnp.einsum('nsr,smr->nsm', z, C)
            topv, topi = jax.lax.top_k(scores, K)
            w = jax.nn.softmax(topv, axis=-1)
            sidx = jnp.arange(S)[None, :, None]
            W1g = W1[sidx, topi]
            b1g = b1[sidx, topi]
            W2g = W2[sidx, topi]
            b2g = b2[sidx, topi]
            h = jax.nn.gelu(jnp.einsum('nsr,nskrh->nskh', z, W1g) + b1g)
            yl = jnp.einsum('nskh,nskhr->nskr', h, W2g) + b2g
            comb = jnp.einsum('nskr,nsk->nsr', yl, w)
            comb = comb.reshape(xf.shape[0], S * R)
            out = jax.nn.gelu(comb @ G1 + g1b) @ G2 + g2b
            return out.reshape(shp)
        key = jax.random.key(seed)
        k = jax.random.split(key, 8)
        rn = lambda kk, shape, s: jax.random.normal(kk, shape, dtype=jnp.float32) * s
        return {'x': rn(k[0], (B, T, D), 1.0), 'P': rn(k[1], (S, D, R), D ** (-0.5)), 'C': rn(k[2], (S, M, R), R ** (-0.5)), 'W1': rn(k[3], (S, M, R, H), R ** (-0.5)), 'b1': jnp.zeros((S, M, H), jnp.float32), 'W2': rn(k[4], (S, M, H, R), H ** (-0.5)), 'b2': jnp.zeros((S, M, R), jnp.float32), 'G1': rn(k[5], (S * R, G), (S * R) ** (-0.5)), 'g1b': jnp.zeros((G,), jnp.float32), 'G2': rn(k[6], (G, D), G ** (-0.5)), 'g2b': jnp.zeros((D,), jnp.float32)}
    _L0_ffn_all = _L0_ffn_setup()
    _L0_ffn_in = {k: v for k, v in _L0_ffn_all.items() if k in ('P', 'C', 'W1', 'b1', 'W2', 'b2', 'G1', 'g1b', 'G2', 'g2b')}
    del _L0_ffn_all
    return {'x': x, 'L0_tok_weight': _L0_tok_in['weight'], 'L0_attn_W_Q': _L0_attn_in['W_Q'], 'L0_attn_b_Q': _L0_attn_in['b_Q'], 'L0_attn_W_K': _L0_attn_in['W_K'], 'L0_attn_b_K': _L0_attn_in['b_K'], 'L0_attn_W_V': _L0_attn_in['W_V'], 'L0_attn_b_V': _L0_attn_in['b_V'], 'L0_attn_W_O': _L0_attn_in['W_O'], 'L0_attn_b_O': _L0_attn_in['b_O'], 'L0_ffn_P': _L0_ffn_in['P'], 'L0_ffn_C': _L0_ffn_in['C'], 'L0_ffn_W1': _L0_ffn_in['W1'], 'L0_ffn_b1': _L0_ffn_in['b1'], 'L0_ffn_W2': _L0_ffn_in['W2'], 'L0_ffn_b2': _L0_ffn_in['b2'], 'L0_ffn_G1': _L0_ffn_in['G1'], 'L0_ffn_g1b': _L0_ffn_in['g1b'], 'L0_ffn_G2': _L0_ffn_in['G2'], 'L0_ffn_g2b': _L0_ffn_in['g2b']}

def reference(x, L0_tok_weight, L0_attn_W_Q, L0_attn_b_Q, L0_attn_W_K, L0_attn_b_K, L0_attn_W_V, L0_attn_b_V, L0_attn_W_O, L0_attn_b_O, L0_ffn_P, L0_ffn_C, L0_ffn_W1, L0_ffn_b1, L0_ffn_W2, L0_ffn_b2, L0_ffn_G1, L0_ffn_g1b, L0_ffn_G2, L0_ffn_g2b):
    import jax
    import jax.numpy as jnp

    def _L0_tok_ref(indices, weight):
        import jax, jax.numpy as jnp
        import numpy as np
        NF4_LEVELS = jnp.array([-1.0, -0.6961928009986877, -0.5250730514526367, -0.39491748809814453, -0.28444138169288635, -0.18477343022823334, -0.09105003625154495, 0.0, 0.07958029955625534, 0.16093020141124725, 0.24611230194568634, 0.33791524171829224, 0.44070982933044434, 0.5626170039176941, 0.8481764793395996, 1.0], dtype=jnp.float32)
        NF4_MIDPOINTS = (NF4_LEVELS[1:] + NF4_LEVELS[:-1]) * 0.5
        BLOCK_SIZE = 64
        SIGMA_FACTOR = 3.0
        EPS = 1e-12

        def fake_quantize_tcfp12(x, block_size=BLOCK_SIZE, nf4_residual=True, nf_aware_scaling=True, sigma_factor=SIGMA_FACTOR):
            shape = x.shape
            xb = x.reshape(-1, block_size)
            absmax = jnp.max(jnp.abs(xb), axis=1, keepdims=True)
            if nf_aware_scaling:
                std = jnp.std(xb, axis=1, keepdims=True)
                scale = jnp.minimum(absmax, sigma_factor * std)
            else:
                scale = absmax
            scale = jnp.maximum(scale, EPS)
            q = jnp.clip(jnp.round(xb / scale * 127.0), -127.0, 127.0)
            main = q * (scale / 127.0)
            res = xb - main
            if nf4_residual:
                rmax = jnp.maximum(jnp.max(jnp.abs(res), axis=1, keepdims=True), EPS)
                rn = res / rmax
                idx = jnp.searchsorted(NF4_MIDPOINTS, rn)
                rq = NF4_LEVELS[idx] * rmax
            else:
                rmax = jnp.maximum(jnp.max(jnp.abs(res), axis=1, keepdims=True), EPS)
                rq = jnp.clip(jnp.round(res / rmax * 7.0), -7.0, 7.0) * (rmax / 7.0)
            return (main + rq).reshape(shape)

        def ste_fake_quantize(x):
            return x + jax.lax.stop_gradient(fake_quantize_tcfp12(x) - x)
        raw = weight[indices]
        return ste_fake_quantize(raw)

    def _L0_attn_ref(normalized_resid_pre, W_Q, b_Q, W_K, b_K, W_V, b_V, W_O, b_O):
        import jax, jax.numpy as jnp
        import numpy as np
        import math
        D_MODEL, N_HEADS, D_HEAD, SEQ, BATCH = (192, 12, 64, 256, 8)
        INIT_RANGE = 0.02
        x = normalized_resid_pre
        q = jnp.einsum('bsd,hde->bshe', x, W_Q) + b_Q
        k = jnp.einsum('bsd,hde->bshe', x, W_K) + b_K
        v = jnp.einsum('bsd,hde->bshe', x, W_V) + b_V
        scores = jnp.einsum('bqhe,bkhe->bhqk', q, k) / math.sqrt(D_HEAD)
        s = x.shape[1]
        causal = jnp.tril(jnp.ones((s, s), dtype=bool))
        scores = jnp.where(causal[None, None], scores, -jnp.inf)
        pattern = jax.nn.softmax(scores, axis=-1)
        pattern = jnp.where(jnp.isnan(pattern), 0.0, pattern)
        z = jnp.einsum('bhqk,bkhe->bqhe', pattern, v)
        attn_out = jnp.einsum('bqhe,hed->bqd', z, W_O) + b_O
        return attn_out

    def _L0_ffn_ref(x, P, C, W1, b1, W2, b2, G1, g1b, G2, g2b):
        import jax, jax.numpy as jnp
        import numpy as np
        B, T, D = (2, 512, 192)
        S, R, M, K = (8, 16, 64, 4)
        H, G = (32, 64)

        def _ssinf3(x, P, C, W1, b1, W2, b2, G1, g1b, G2, g2b):
            shp = x.shape
            xf = x.reshape(-1, shp[-1])
            z = jnp.einsum('nd,sdr->nsr', xf, P)
            scores = jnp.einsum('nsr,smr->nsm', z, C)
            topv, topi = jax.lax.top_k(scores, K)
            w = jax.nn.softmax(topv, axis=-1)
            sidx = jnp.arange(S)[None, :, None]
            W1g = W1[sidx, topi]
            b1g = b1[sidx, topi]
            W2g = W2[sidx, topi]
            b2g = b2[sidx, topi]
            h = jax.nn.gelu(jnp.einsum('nsr,nskrh->nskh', z, W1g) + b1g)
            yl = jnp.einsum('nskh,nskhr->nskr', h, W2g) + b2g
            comb = jnp.einsum('nskr,nsk->nsr', yl, w)
            comb = comb.reshape(xf.shape[0], S * R)
            out = jax.nn.gelu(comb @ G1 + g1b) @ G2 + g2b
            return out.reshape(shp)
        return _ssinf3(x, P, C, W1, b1, W2, b2, G1, g1b, G2, g2b)
    h = _L0_tok_ref(x, L0_tok_weight)
    h = h + _L0_attn_ref(_layernorm(h, axis=-1), L0_attn_W_Q, L0_attn_b_Q, L0_attn_W_K, L0_attn_b_K, L0_attn_W_V, L0_attn_b_V, L0_attn_W_O, L0_attn_b_O)
    h = h + _L0_ffn_ref(_layernorm(h, axis=-1), L0_ffn_P, L0_ffn_C, L0_ffn_W1, L0_ffn_b1, L0_ffn_W2, L0_ffn_b2, L0_ffn_G1, L0_ffn_g1b, L0_ffn_G2, L0_ffn_g2b)
    return h

_drawn_inputs = setup_inputs


def setup_inputs(seed=0):
    import zlib

    import numpy as np

    out = dict(_drawn_inputs(seed))
    spreads = {'L0_attn_b_Q': (0.0, 0.8),
     'L0_attn_b_K': (0.0, 0.8),
     'L0_attn_b_V': (0.0, 0.1),
     'L0_attn_b_O': (0.0, 0.1),
     'L0_ffn_b1': (0.0, 0.422),
     'L0_ffn_b2': (0.0, 0.274),
     'L0_ffn_g1b': (0.0, 0.1),
     'L0_ffn_g2b': (0.0, 0.1)}
    factors = {'L0_attn_W_Q': 8.0, 'L0_attn_W_K': 8.0, 'L0_attn_W_V': 3.455}
    for name, (base, spread) in spreads.items():
        noise = np.random.default_rng([zlib.crc32(name.encode()), seed]).standard_normal(out[name].shape)
        drawn = base * np.exp(spread * noise) if base else spread * noise
        out[name] = jnp.asarray(drawn.astype(out[name].dtype))
    for name, factor in factors.items():
        out[name] = (out[name] * factor).astype(out[name].dtype)
    return out
```

```python
import concourse.bass as bass
from concourse import mybir
from contextlib import ExitStack

F32 = mybir.dt.float32
F32R = mybir.dt.float32r
F16 = mybir.dt.float16
BF16 = mybir.dt.bfloat16
I32 = mybir.dt.int32
U32 = mybir.dt.uint32
ALU = mybir.AluOpType
ACT = mybir.ActivationFunctionType
AX = mybir.AxisListType

P = 128
B, T, D = 2, 2048, 192
DLO = D - P
NT = B * T // P
GT = 4
NG = NT // GT
GW = GT * D
GTOK = GT * P
H, E = 12, 64
NP = H // 2
KT = T // P
S, R, M, HID = 8, 16, 64, 32
NJ = M * HID // P
NQ = 4
GH = 64
TOPK = 4
VOCAB = 50257

QB = 64
NB = GW // QB
BT = D // QB
QEPS = 1e-12
LNEPS = 1e-5
ROUND = 12582912.0
NEG = -3.0e38
MASKED = -1.0e30
NF4 = [-1.0, -0.6961928009986877, -0.5250730514526367, -0.39491748809814453, -0.28444138169288635,
       -0.18477343022823334, -0.09105003625154495, 0.0, 0.07958029955625534, 0.16093020141124725,
       0.24611230194568634, 0.33791524171829224, 0.44070982933044434, 0.5626170039176941,
       0.8481764793395996, 1.0]


def nf4_midpoints():
    import numpy as np
    v = np.array(NF4, np.float32)
    return [float(x) for x in (v[1:] + v[:-1]) * np.float32(0.5)]


MID = nf4_midpoints()
STEP = [NF4[i + 1] - NF4[i] for i in range(15)]


def tower(nc, x, tok_w, w_q, b_q, w_k, b_k, w_v, b_v, w_o, b_o,
          f_p, f_c, f_w1, f_b1, f_w2, f_b2, f_g1, f_g1b, f_g2, f_g2b, out, stages=3):
    ctx = ExitStack()
    with ctx:
        def sb(name, shape, dt=F32):
            return ctx.enter_context(nc.sbuf_tensor(name, shape, dt))

        def sem(name):
            return ctx.enter_context(nc.semaphore(name))

        xT_dram = nc.dram_tensor("xT_scratch", (D, B * T), F32, kind="Internal").ap()

        h_all = sb("h_all", [P, NT * D])
        ident = sb("ident", [P, P])
        idx = sb("idx", [P, NT], I32)
        bo_bc = sb("bo_bc", [P, D])
        banks = ctx.enter_context(nc.psum_tensor("banks", [P, 8 * 512], F32))
        psum = [banks[:, i * 512:(i + 1) * 512] for i in range(8)]

        stage_embed(nc, ctx, x, tok_w, b_o, h_all, ident, idx, bo_bc, psum, xT_dram)
        if stages >= 2:
            stage_attention(nc, w_q, b_q, w_k, b_k, w_v, b_v, w_o, h_all, ident, psum, xT_dram)
        if stages >= 3:
            stage_experts(nc, f_p, f_c, f_w1, f_b1, f_w2, f_b2, f_g1, f_g1b, f_g2, f_g2b,
                          h_all, ident, banks, psum, out)
        else:
            with nc.semaphore("dbg") as dbg, nc.Block() as block:
                @block.sync
                def _(sp):
                    sp.dma_start(out.rearrange("(n p) d -> p n d", p=P),
                                 h_all[:, :].rearrange("p (n d) -> p n d", d=D)).then_inc(dbg, 16)
                    sp.wait_ge(dbg, 16)


def normalise_chain(dve, link, src, c, sq, small, sqrt_asked, sqrt_done, asked, done):
    mean, var, rstd, t = (small[:, GT * i:GT * i + GT] for i in range(4))
    wide = lambda a: a.unsqueeze(2).to_broadcast([P, GT, D])
    link(dve.tensor_reduce(mean, src, AX.X, ALU.add))
    link(dve.tensor_scalar(mean, mean, 1.0 / D, None, ALU.mult))
    link(dve.tensor_tensor(c, src, wide(mean), ALU.subtract))
    link(dve.tensor_tensor(sq, c, c, ALU.mult))
    link(dve.tensor_reduce(var, sq, AX.X, ALU.add))
    dve.tensor_scalar(var, var, 1.0 / D, LNEPS, ALU.mult, ALU.add).then_inc(sqrt_asked, 1)
    dve.wait_ge(sqrt_done, done)
    link(dve.reciprocal(rstd, rstd))
    link(dve.tensor_tensor(t, rstd, rstd, ALU.mult))
    link(dve.tensor_tensor(t, t, var, ALU.mult))
    link(dve.tensor_scalar(t, t, -0.5, 1.5, ALU.mult, ALU.add))
    link(dve.tensor_tensor(rstd, rstd, t, ALU.mult))


def stage_embed(nc, ctx, x, tok_w, b_o, h_all, ident, idx, bo_bc, psum, xT_dram):
    with ExitStack() as own:
        def sb(name, shape, dt=F32):
            return own.enter_context(nc.sbuf_tensor(name, shape, dt))

        def sem(name):
            return own.enter_context(nc.semaphore(name))

        raw = sb("raw", [P, NT * D])
        xg = sb("xg", [P, GW])
        main = sb("main", [P, GW])
        work = sb("work", [P, GW])
        res = sb("res", [P, GW])
        gate = sb("gate", [P, GW])
        level = sb("level", [P, GW])
        xn = sb("xn", [P, GW])
        xs_hi = sb("xs_hi", [P, GTOK])
        xs_lo = sb("xs_lo", [DLO, GTOK])
        blk = sb("blk", [P, 8 * NB])
        small = sb("small", [P, 4 * GT])

        idx_in, rows_in, bias_in = sem("idx_in"), sem("rows_in"), sem("bias_in")
        const_ready = sem("const_ready")
        step = sem("embed_step")
        qvar_ready, qstd_ready = sem("qvar_ready"), sem("qstd_ready")
        lnvar_ready, lnstd_ready = sem("lnvar_ready"), sem("lnstd_ready")
        xn_ready, xT_turned, xT_copied, xT_stored = (sem("xn_ready"), sem("xT_turned"),
                                                     sem("xT_copied"), sem("xT_stored"))
        STEPS = 69

        block = own.enter_context(nc.Block())

        @block.sync
        def _(sp):
            sp.sem_inc(xT_stored, 32)
            sp.dma_start(idx[:, :], x).then_inc(idx_in, 16)
            sp.dma_start(bo_bc[:, :], b_o.rearrange("(a d) -> a d", a=1).to_broadcast([P, D])).then_inc(bias_in, 16)
            with sp.Fori(0, NG) as g:
                sp.wait_ge(xT_copied, g + 2)
                sp.dma_start(xT_dram[0:P, bass.ds(g * GTOK, GTOK)], xs_hi[:, :]).then_inc(xT_stored, 16)
                sp.dma_start(xT_dram[P:D, bass.ds(g * GTOK, GTOK)], xs_lo[:, :]).then_inc(xT_stored, 16)
            sp.wait_ge(xT_stored, 32 * NG + 32)

        @block.gpsimd
        def _(pool):
            pool.memset(ident[:, :], 0.0).then_inc(const_ready, 1)
            pool.wait_ge(const_ready, 1)
            pool.affine_select(out=ident[:, :], in_=ident[:, :], pattern=[[-1, P]], compare_op=ALU.not_equal,
                               fill=1.0, base=0, channel_multiplier=1).then_inc(const_ready, 1)
            pool.wait_ge(idx_in, 16)
            for n in range(NT):
                pool.indirect_dma_start(out=raw[:, n * D:(n + 1) * D], out_offset=None, in_=tok_w,
                                        in_offset=bass.IndirectOffsetOnAxis(ap=idx[:, n:n + 1], axis=0),
                                        bounds_check=VOCAB - 1, oob_is_err=False).then_inc(rows_in, 16)

        @block.vector
        def _(dve):
            dve.wait_ge(rows_in, 16 * NT)
            dve.wait_ge(bias_in, 16)
            blocks = lambda a: a.rearrange("p (n q) -> p n q", q=QB)
            wide = lambda a: a.unsqueeze(2).to_broadcast([P, NB, QB])
            amax, var, s, r, t, scale, s127, rmax = (blk[:, NB * i:NB * i + NB] for i in range(8))
            with dve.Fori(0, NG) as g:
                n = [0]

                def link(ins):
                    n[0] += 1
                    ins.then_inc(step, 1)
                    dve.wait_ge(step, g * STEPS + n[0])

                X = xg[:, :]
                link(dve.tensor_scalar(X, raw[:, bass.ds(g * GW, GW)], 1.0, None, ALU.mult))
                Xb, Wb, Mb, Rb, Gb, Lb = map(blocks, (X, work[:, :], main[:, :], res[:, :], gate[:, :], level[:, :]))
                link(dve.tensor_reduce(amax, Xb, AX.X, ALU.max, apply_absolute_value=True))
                link(dve.tensor_reduce(s, Xb, AX.X, ALU.add))
                link(dve.tensor_scalar(s, s, 1.0 / QB, None, ALU.mult))
                link(dve.tensor_tensor(Wb, Xb, wide(s), ALU.subtract))
                link(dve.tensor_tensor(Wb, Wb, Wb, ALU.mult))
                link(dve.tensor_reduce(var, Wb, AX.X, ALU.add))
                dve.tensor_scalar(var, var, 1.0 / QB, None, ALU.mult).then_inc(qvar_ready, 1)
                dve.wait_ge(qstd_ready, g + 1)
                link(dve.tensor_scalar(s, s, 1e-18, None, ALU.max))
                link(dve.reciprocal(r, s))
                link(dve.tensor_tensor(r, r, var, ALU.mult))
                link(dve.tensor_tensor(s, s, r, ALU.add))
                link(dve.tensor_scalar(s, s, 1.5, None, ALU.mult))
                link(dve.tensor_tensor(s, s, amax, ALU.min))
                link(dve.tensor_scalar(scale, s, QEPS, None, ALU.max))
                link(dve.reciprocal(r, scale))
                link(dve.tensor_scalar(s127, scale, 1.0 / 127.0, None, ALU.mult))
                link(dve.tensor_tensor(Wb, Xb, wide(r), ALU.mult))
                link(dve.tensor_scalar(work[:, :], work[:, :], 127.0, ROUND, ALU.mult, ALU.add))
                link(dve.tensor_scalar(work[:, :], work[:, :], ROUND, 127.0, ALU.subtract, ALU.min))
                link(dve.scalar_tensor_tensor(Mb, Wb, -127.0, wide(s127), ALU.max, ALU.mult))
                link(dve.tensor_tensor(res[:, :], X, main[:, :], ALU.subtract))
                link(dve.tensor_reduce(rmax, Rb, AX.X, ALU.max, apply_absolute_value=True))
                link(dve.tensor_scalar(rmax, rmax, QEPS, None, ALU.max))
                link(dve.reciprocal(t, rmax))
                link(dve.tensor_tensor(Rb, Rb, wide(t), ALU.mult))
                link(dve.tensor_scalar(level[:, :], res[:, :], MID[14], STEP[14], ALU.is_gt, ALU.mult))
                for j in range(13, -1, -1):
                    g_j = (gate, work)[j % 2]
                    link(dve.tensor_scalar(g_j[:, :], res[:, :], MID[j], None, ALU.is_gt))
                    link(dve.scalar_tensor_tensor(level[:, :], level[:, :], STEP[j], g_j[:, :], ALU.add, ALU.mult))
                link(dve.scalar_tensor_tensor(Lb, Lb, NF4[0], wide(rmax), ALU.add, ALU.mult))
                link(dve.tensor_tensor(level[:, :], level[:, :], main[:, :], ALU.add))
                link(dve.tensor_tensor(level[:, :], level[:, :], X, ALU.subtract))
                link(dve.tensor_tensor(level[:, :], level[:, :], X, ALU.add))
                tok = lambda a: a.rearrange("p (n d) -> p n d", d=D)
                link(dve.tensor_tensor(tok(h_all[:, bass.ds(g * GW, GW)]), tok(level[:, :]),
                                       bo_bc[:, :].unsqueeze(1).to_broadcast([P, GT, D]), ALU.add))
                normalise_chain(dve, link, tok(level[:, :]), tok(work[:, :]), tok(main[:, :]), small,
                                lnvar_ready, lnstd_ready, g + 1, g + 1)
                dve.wait_ge(xT_turned, g + 1)
                dve.tensor_tensor(tok(xn[:, :]), tok(work[:, :]),
                                  small[:, 2 * GT:3 * GT].unsqueeze(2).to_broadcast([P, GT, D]),
                                  ALU.mult).then_inc(xn_ready, 1)
                assert n[0] == STEPS
                dve.wait_ge(xn_ready, g + 1)

        @block.scalar
        def _(act):
            act.sem_inc(xT_copied, 1)
            with act.Fori(0, NG) as g:
                act.wait_ge(qvar_ready, g + 1)
                act.activation(blk[:, 2 * NB:3 * NB], blk[:, NB:2 * NB], ACT.Sqrt).then_inc(qstd_ready, 1)
                act.wait_ge(lnvar_ready, g + 1)
                act.activation(small[:, 2 * GT:3 * GT], small[:, GT:2 * GT], ACT.Sqrt).then_inc(lnstd_ready, 1)
                act.wait_ge(xT_turned, g + 2)
                act.wait_ge(xT_stored, 32 * g + 32)
                act.activation(xs_hi[:, :], psum[0][:, :], ACT.Copy)
                act.activation(xs_lo[:, :], psum[1][0:DLO, :], ACT.Copy).then_inc(xT_copied, 1)

        @block.tensor
        def _(pe):
            pe.sem_inc(xT_turned, 1)
            pe.wait_ge(const_ready, 2)
            with pe.Fori(0, NG) as g:
                pe.wait_ge(xn_ready, g + 1)
                pe.wait_ge(xT_copied, g + 1)
                for c in range(GT):
                    pe.transpose(psum[0][:, c * P:(c + 1) * P], xn[:, c * D:c * D + P], ident[:, :])
                    last = pe.transpose(psum[1][0:DLO, c * P:(c + 1) * P], xn[:, c * D + P:(c + 1) * D], ident[:, :])
                last.then_inc(xT_turned, 1)


def stage_attention(nc, w_q, b_q, w_k, b_k, w_v, b_v, w_o, h_all, ident, psum, xT_dram):
    CH = 512
    PC = CH // P
    CHUNKS = [i // PC + 1 for i in range(KT)]
    NC = sum(CHUNKS)
    BEFORE = [sum(CHUNKS[:i]) for i in range(KT)]
    ITEMS = 6 + NC + KT
    OF_DVE = ITEMS - 2
    SLOTS = 3
    LSLOTS = 8
    STEPS = 2 * KT
    with ExitStack() as own:
        def sb(name, shape, dt=F32):
            return own.enter_context(nc.sbuf_tensor(name, shape, dt))

        def sem(name):
            return own.enter_context(nc.semaphore(name))

        xt_hi = sb("xt_hi", [P, T])
        xt_lo = sb("xt_lo", [P, T // 2])
        w_hi = sb("w_hi", [P, 3, P])
        w_lo = sb("w_lo", [P, 3, P])
        wo = sb("wo", [P, D])
        bq, bk, bv_bc = sb("bq", [P, 1]), sb("bk", [P, 1]), sb("bv_bc", [P, P])
        qT, kT, v = sb("qT", [P, T]), sb("kT", [P, T]), sb("v", [P, KT, P])
        probs = sb("probs", [P, SLOTS, 2, T])
        probsT = sb("probsT", [P, 2, 2, KT, P])
        oT = sb("oT", [P, 2, P])
        mask = sb("mask", [P, P])
        part = sb("part", [P, 2, KT // PC + 1])
        negmax = sb("negmax", [P, SLOTS, 2])
        total = sb("total", [P, LSLOTS, 2])
        rtotal = sb("rtotal", [P, LSLOTS, 2])

        mask_ready = sem("mask_ready")
        x_in, w_in, wo_in = sem("x_in"), sem("w_in"), sem("wo_in")
        v_copied, k_copied = sem("v_copied"), sem("k_copied")
        filled, emptied = sem("ring_filled"), sem("ring_emptied")
        max_ready, exp_done = sem("max_ready"), sem("exp_done")
        turned = [sem("turned_a"), sem("turned_b")]
        copied = [sem("copied_a"), sem("copied_b")]
        weighed, oT_copied = sem("weighed"), sem("oT_copied")
        step = sem("attn_step")

        pairs = [("q", 0), ("q", 1), ("k", 0), ("k", 1), ("v", 0), ("v", 1)]
        order = list(pairs)
        for i in range(2):
            order += [("s", i, c) for c in range(CHUNKS[i])]
        for i in range(KT + 2):
            if i + 2 < KT:
                order += [("s", i + 2, c) for c in range(CHUNKS[i + 2])]
            if i >= 2:
                order.append(("o", i - 2))
        assert len(order) == ITEMS and ITEMS % 2 == 0
        place = {item: n for n, item in enumerate(order)}

        def score_width(i, c):
            return min(CH, (i + 1) * P - c * CH)

        block = own.enter_context(nc.Block())

        @block.gpsimd
        def _(pool):
            pool.memset(mask[:, :], 0.0).then_inc(mask_ready, 1)
            pool.wait_ge(mask_ready, 1)
            pool.affine_select(out=mask[:, :], in_=mask[:, :], pattern=[[-1, P]], compare_op=ALU.is_ge,
                               fill=MASKED, base=0, channel_multiplier=1).then_inc(mask_ready, 1)

        @block.sync
        def _(sp):
            sp.sem_inc(v_copied, 1)
            sp.sem_inc(k_copied, 2)
            with sp.Fori(0, B) as b:
                sp.wait_ge(v_copied, b * NP + 1)
                sp.dma_start(xt_hi[:, :], xT_dram[0:P, bass.ds(b * T, T)]).then_inc(x_in, 16)
                for half in range(2):
                    sp.dma_start(xt_lo[half * DLO:(half + 1) * DLO, :],
                                 xT_dram[P:D, bass.ds(b * T + half * (T // 2), T // 2)]).then_inc(x_in, 16)
                with sp.Fori(0, NP) as p:
                    it = b * NP + p
                    sp.wait_ge(v_copied, it + 1)
                    sp.wait_ge(k_copied, 2 * it + 2)
                    for n, w in enumerate((w_q, w_k, w_v)):
                        wd = w.rearrange("h d e -> d h e")
                        for dst, d0 in ((w_hi[:, n, :], 0), (w_lo[0:DLO, n, :], P), (w_lo[DLO:P, n, :], P)):
                            k = dst.shape[0]
                            sp.dma_start(dst.rearrange("d (h e) -> d h e", e=E),
                                         wd[d0:d0 + k, bass.ds(2 * p, 2), :]).then_inc(w_in, 16)
                    for dst, src in ((bq, b_q), (bk, b_k)):
                        sp.dma_start(dst[:, :], src.rearrange("h (e a) -> (h e) a", a=1)[bass.ds(p * P, P), :])\
                          .then_inc(w_in, 16)
                    sp.dma_start(bv_bc[:, :], b_v.rearrange("(a g) e -> a (g e)", g=2)[bass.ds(p, 1), :]
                                 .to_broadcast([P, P])).then_inc(w_in, 16)
                    sp.wait_ge(emptied, it * OF_DVE + 2)
                    sp.dma_start(wo[:, :], w_o.rearrange("h e d -> (h e) d")[bass.ds(p * P, P), :])\
                      .then_inc(wo_in, 16)

        @block.tensor
        def _(pe):
            with pe.Fori(0, B) as b, pe.Fori(0, NP) as p:
                it = b * NP + p

                def slot_free(n):
                    if n < 2:
                        pe.wait_ge(emptied, it * OF_DVE + n + 1)
                    elif order[n - 2][0] == "k":
                        pe.wait_ge(k_copied, it * 2 + 2 + order[n - 2][1] + 1)
                    else:
                        read = sum(o[0] != "k" for o in order[:n - 1])
                        pe.wait_ge(emptied, it * OF_DVE + read + 2)
                    return psum[2 * (n % 2)], psum[2 * (n % 2) + 1]

                def project(kind, c):
                    n = place[(kind, c)]
                    banks = slot_free(n)
                    if kind == "v":
                        for h in range(2):
                            for k in range(PC):
                                t = (2 * h + c) * PC + k
                                pe.matmul(banks[h][:, k * P:(k + 1) * P], xt_hi[:, t * P:(t + 1) * P],
                                          w_hi[:, 2, :], start=(k == 0), stop=False, skip_group_check=True)
                        for k in range(PC):
                            for h in range(2):
                                t = c * PC + k
                                rows = slice(h * DLO, (h + 1) * DLO)
                                last = pe.matmul(banks[h][:, k * P:(k + 1) * P], xt_lo[rows, t * P:(t + 1) * P],
                                                 w_lo[rows, 2, :], start=False, stop=True, skip_group_check=True)
                    else:
                        w = "qk".index(kind)
                        for h in range(2):
                            t = (2 * h + c) * CH
                            pe.matmul(banks[h][:, :], w_hi[:, w, :], xt_hi[:, t:t + CH], start=True, stop=False)
                        for h in range(2):
                            rows = slice(h * DLO, (h + 1) * DLO)
                            last = pe.matmul(banks[h][:, :], w_lo[rows, w, :], xt_lo[rows, c * CH:(c + 1) * CH],
                                             start=False, stop=True)
                    last.then_inc(filled, 1)

                def score(i, c):
                    banks = slot_free(place[("s", i, c)])
                    w = score_width(i, c)
                    for h in range(2):
                        rows = slice(h * E, (h + 1) * E)
                        last = pe.matmul(banks[h][:, 0:w], qT[rows, i * P:(i + 1) * P],
                                         kT[rows, c * CH:c * CH + w], start=True, stop=True)
                    last.then_inc(filled, 1)

                def turn(i, c):
                    for h in range(2):
                        if c == 0:
                            pe.wait_ge(exp_done, it * 2 * KT + 2 * i + h + 1)
                        pe.wait_ge(copied[h], it * NC + BEFORE[i] + c + 1)
                        for k in range(c * PC, min(i + 1, (c + 1) * PC)):
                            last = pe.transpose(psum[4 + h][:, (k % PC) * P:(k % PC + 1) * P],
                                                probs[:, i % SLOTS, h, k * P:(k + 1) * P], ident[:, :])
                        last.then_inc(turned[h], 1)

                def weigh(i, c):
                    for h in range(2):
                        pe.wait_ge(copied[h], it * NC + BEFORE[i] + c + 2)
                    for k in range(c * PC, min(i + 1, (c + 1) * PC)):
                        for h in range(2):
                            rows = slice(h * E, (h + 1) * E)
                            last = pe.matmul(psum[6 + i % 2][rows, 0:P], v[:, k, rows], probsT[:, i % 2, h, k, :],
                                             start=(k == 0), stop=(k == i))
                    if (c + 1) * PC > i:
                        last.then_inc(weighed, 1)

                def output(i):
                    banks = slot_free(place[("o", i)])
                    if i == 0:
                        pe.wait_ge(wo_in, it * 16 + 16)
                    pe.wait_ge(oT_copied, it * KT + i + 1)
                    for h in range(2):
                        rows = slice(h * E, (h + 1) * E)
                        last = pe.matmul(banks[h][:, 0:D], oT[rows, i % 2, :], wo[rows, :], start=True, stop=True)
                    last.then_inc(filled, 1)

                pe.wait_ge(x_in, b * 48 + 48)
                pe.wait_ge(w_in, it * (12 * 16) + 12 * 16)
                for kind, c in pairs:
                    project(kind, c)
                pe.wait_ge(emptied, it * OF_DVE + 2 + 2)
                pe.wait_ge(k_copied, it * 2 + 2 + 2)
                for i in range(2):
                    for c in range(CHUNKS[i]):
                        score(i, c)
                for i in range(KT + 2):
                    for c in range(KT // PC):
                        if i + 2 < KT and c < CHUNKS[i + 2]:
                            score(i + 2, c)
                        if i < KT and c < CHUNKS[i]:
                            turn(i, c)
                        if 1 <= i <= KT and c < CHUNKS[i - 1]:
                            weigh(i - 1, c)
                    if i >= 2:
                        output(i - 2)

        @block.vector
        def _(dve):
            dve.wait_ge(mask_ready, 2)
            dve.sem_inc(max_ready, 1)
            dve.sem_inc(emptied, 2)
            dve.sem_inc(copied[1], 1)
            with dve.Fori(0, B) as b, dve.Fori(0, NP) as p:
                it = b * NP + p
                steps = [0]

                def link(ins):
                    steps[0] += 1
                    ins.then_inc(step, 1)
                    dve.wait_ge(step, it * STEPS + steps[0])

                def item(*key):
                    n = place[key]
                    dve.wait_ge(filled, it * ITEMS + n + 1)
                    return psum[2 * (n % 2)], psum[2 * (n % 2) + 1]

                def take_scores(i, c):
                    if c == 0:
                        dve.wait_ge(max_ready, it * KT + i + 1)
                    banks = item("s", i, c)
                    w = score_width(i, c)
                    diag = c == CHUNKS[i] - 1
                    whole = w - P if diag else w
                    if not whole:
                        dve.memset(part[:, :, c:c + 1], NEG)
                    for h in range(2):
                        dst = probs[:, i % SLOTS, h, c * CH:c * CH + w]
                        if whole:
                            last = dve.tensor_scalar(dst[:, 0:whole], banks[h][:, 0:whole], 1.0, None, ALU.mult,
                                                     ALU.max, accum_out=part[:, h, c:c + 1])
                            if not diag and h == 1:
                                last.then_inc(emptied, 1)
                        if diag:
                            n = c + 1
                            last = dve.tensor_tensor_reduce(dst[:, whole:w], banks[h][:, whole:w], mask[:, :],
                                                            1.0, NEG, ALU.add, ALU.max, part[:, h, n:n + 1])
                            if h == 1:
                                last.then_inc(emptied, 1)
                    if diag:
                        dve.wait_ge(emptied, it * OF_DVE + 2 + sum(o[0] != "k" for o in order[:place[("s", i, c)] + 1]))
                        dve.tensor_reduce(negmax[:, i % SLOTS, :], part[:, :, 0:n + 1], AX.X, ALU.max,
                                          negate=True).then_inc(max_ready, 1)

                def take_transposes(i, c):
                    dve.wait_ge(turned[1], it * NC + BEFORE[i] + c + 1)
                    a, z = c * PC, min(i + 1, (c + 1) * PC)
                    dve.tensor_copy(probsT[:, i % 2, 1, a:z, :],
                                    psum[5][:, 0:(z - a) * P].rearrange("p (k q) -> p k q", q=P))\
                       .then_inc(copied[1], 1)

                def take_output(i):
                    dve.wait_ge(exp_done, it * 2 * KT + 2 * i + 2)
                    link(dve.reciprocal(rtotal[:, i % LSLOTS, :], total[:, i % LSLOTS, :]))
                    banks = item("o", i)
                    h_tile = h_all[:, bass.ds(b * (KT * D) + i * D, D)]
                    link(dve.scalar_tensor_tensor(h_tile, banks[0][:, 0:D], rtotal[:, i % LSLOTS, 0:1], h_tile,
                                                  ALU.mult, ALU.add))
                    dve.scalar_tensor_tensor(h_tile, banks[1][:, 0:D], rtotal[:, i % LSLOTS, 1:2], h_tile,
                                             ALU.mult, ALU.add).then_inc(emptied, 1)

                dve.wait_ge(w_in, it * (12 * 16) + 12 * 16)
                for c in range(2):
                    banks = item("q", c)
                    for h in range(2):
                        t = (2 * h + c) * CH
                        last = dve.tensor_scalar(qT[:, t:t + CH], banks[h][:, :], bq[:, 0:1], E ** -0.5,
                                                 ALU.add, ALU.mult)
                    last.then_inc(emptied, 1)
                for c in range(2):
                    banks = item("v", c)
                    for h in range(2):
                        t = (2 * h + c) * PC
                        last = dve.tensor_tensor(v[:, t:t + PC, :], banks[h][:, :].rearrange("p (k e) -> p k e", e=P),
                                                 bv_bc[:, :].unsqueeze(1).to_broadcast([P, PC, P]), ALU.add)
                    last.then_inc(emptied, 1)
                dve.wait_ge(emptied, it * OF_DVE + 2 + 4)
                dve.sem_inc(v_copied, 1)
                for i in range(2):
                    for c in range(CHUNKS[i]):
                        take_scores(i, c)
                for i in range(KT + 2):
                    for c in range(KT // PC):
                        if i + 2 < KT and c < CHUNKS[i + 2]:
                            take_scores(i + 2, c)
                        if i < KT and c < CHUNKS[i]:
                            take_transposes(i, c)
                    if i >= 2:
                        take_output(i - 2)
                assert steps[0] == STEPS, steps

        @block.scalar
        def _(act):
            act.sem_inc(copied[0], 1)
            with act.Fori(0, B) as b, act.Fori(0, NP) as p:
                it = b * NP + p

                def exponentials(i):
                    w = (i + 1) * P
                    act.wait_ge(max_ready, it * KT + i + 2)
                    for h in range(2):
                        s = probs[:, i % SLOTS, h, 0:w]
                        act.activation(s, s, ACT.Exp, bias=negmax[:, i % SLOTS, h:h + 1],
                                       accum_out=total[:, i % LSLOTS, h:h + 1]).then_inc(exp_done, 1)

                act.wait_ge(w_in, it * (12 * 16) + 12 * 16)
                for c in range(2):
                    n = place[("k", c)]
                    act.wait_ge(filled, it * ITEMS + n + 1)
                    for h in range(2):
                        t = (2 * h + c) * CH
                        last = act.activation(kT[:, t:t + CH], psum[2 * (n % 2) + h][:, :], ACT.Identity,
                                              bias=bk[:, 0:1])
                    last.then_inc(k_copied, 1)
                exponentials(0)
                exponentials(1)
                for i in range(KT + 1):
                    for c in range(KT // PC):
                        if i < KT and c < CHUNKS[i]:
                            act.wait_ge(turned[0], it * NC + BEFORE[i] + c + 1)
                            a, z = c * PC, min(i + 1, (c + 1) * PC)
                            act.activation(probsT[:, i % 2, 0, a:z, :],
                                           psum[4][:, 0:(z - a) * P].rearrange("p (k q) -> p k q", q=P),
                                           ACT.Copy).then_inc(copied[0], 1)
                    if i >= 1:
                        act.wait_ge(weighed, it * KT + i)
                        act.activation(oT[:, (i - 1) % 2, :], psum[6 + (i - 1) % 2][:, 0:P],
                                       ACT.Copy).then_inc(oT_copied, 1)
                    if i + 2 < KT:
                        exponentials(i + 2)


def stage_experts(nc, f_p, f_c, f_w1, f_b1, f_w2, f_b2, f_g1, f_g1b, f_g2, f_g2b,
                  h_all, ident, banks, psum, out):
    ZPART, WPART = (0, 0, 1), (0, 1, 0)
    ZR = len(ZPART) * R
    KR = ZR + 2
    HALF = 64
    TOP = TOPK + M
    BIG = 3.0e38
    TAKEN = -3.0e38
    NSTEP = 2 * NJ
    WBANKS = 3
    STEPS = 19
    with ExitStack() as own:
        def sb(name, shape, dt=F32):
            return own.enter_context(nc.sbuf_tensor(name, shape, dt))

        def sem(name):
            return own.enter_context(nc.semaphore(name))

        z_dram = nc.dram_tensor("z_scratch", (2, P, GTOK), F32, kind="Internal").ap()

        w1 = sb("w1", [P, NQ, M * HID], F32R)
        w2 = sb("w2", [P, S, NJ, 2 * R])
        b2 = sb("b2", [P, 3, S, 2 * R], BF16)
        pm_hi, pm_lo = sb("pm_hi", [P, S * R]), sb("pm_lo", [DLO, S * R])
        cm = sb("cm", [P, NQ, M], F32R)
        g1, g1b, g2 = sb("g1", [P, GH]), sb("g1b", [GH, 1]), sb("g2", [GH, D])
        g2b_bc = sb("g2b_bc", [P, D])
        ident16 = sb("ident16", [P, P], F16)
        select = sb("select", [P, NJ, P], F16)
        zst = sb("zst", [P, NQ, GTOK], F32R)
        loaded, cleared, split, placed = sem("loaded"), sem("cleared"), sem("split"), sem("placed")
        selected = sem("selected")
        LOADS = 11 + S
        step = sem("route_step")
        lnvar, lnstd = sem("lnvar2"), sem("lnstd2")
        xn_ready, x_turned, x_copied = sem("xn2_ready"), sem("x2_turned"), sem("x2_copied")
        z_done, zh_done, z_split = sem("z_done"), sem("zh_done"), sem("z_split")
        z_stored, z_in = sem("z_stored"), sem("z_in")
        scored, sc_copied = sem("scored"), sem("sc_copied")
        exp_asked, exp_done = sem("exp_asked2"), sem("exp_done2")
        w_ready, w_turned, w_copied = sem("w_ready"), sem("w_turned"), sem("w_copied")
        up_done, gelu_done = sem("up_done"), sem("gelu_done")
        spread, mixed, down_done = sem("spread"), sem("mixed"), sem("down_done")
        comb_ready, g1_done, gh_ready = sem("comb_ready"), sem("g1_done"), sem("gh_ready")
        g2_done, out_ready, out_stored = sem("g2_done"), sem("out_ready"), sem("out_stored")

        with ExitStack() as setup:
            raw1 = setup.enter_context(nc.sbuf_tensor("raw1", [P, M * HID], F32))
            raw1p = setup.enter_context(nc.sbuf_tensor("raw1p", [P, 2, M * HID], F32R))
            rawb = setup.enter_context(nc.sbuf_tensor("rawb", [S, M * HID], F32))
            rawbp = setup.enter_context(nc.sbuf_tensor("rawbp", [S, 2, M * HID], F32R))
            rawc = setup.enter_context(nc.sbuf_tensor("rawc", [P, M], F32))
            rawcp = setup.enter_context(nc.sbuf_tensor("rawcp", [P, 2, M], F32R))
            rawb2 = setup.enter_context(nc.sbuf_tensor("rawb2", [P, S, 2 * R], F32))
            rawb2r = setup.enter_context(nc.sbuf_tensor("rawb2r", [P, S, 2 * R], F32))
            block = setup.enter_context(nc.Block())

            @block.gpsimd
            def _(pool):
                pool.memset(select[:, :, :], 0.0).then_inc(selected, 1)
                pool.memset(w2[:, :, :, :], 0.0).then_inc(cleared, 1)
                pool.memset(rawb2[:, :, :], 0.0).then_inc(cleared, 1)
                pool.tensor_copy(ident16[:, :], ident[:, :])
                for half in range(2):
                    view = select[:, :, :].rearrange("p j (e u) -> p j e u", u=HID)
                    pool.wait_ge(selected, half + 1)
                    pool.affine_select(out=view, in_=view, compare_op=ALU.not_equal, fill=1.0, base=-M * half,
                                       pattern=[[-4, NJ], [-1, 4], [0, HID]], channel_multiplier=1)\
                        .then_inc(selected, 1)

            @block.sync
            def _(sp):
                with nc.allow_non_contiguous_dma(reason="weights, once"):
                    for s in range(S):
                        sp.dma_start(raw1[s * R:(s + 1) * R, :].rearrange("r (m h) -> r m h", h=HID),
                                     f_w1[s].rearrange("m r h -> r m h")).then_inc(loaded, 16)
                    sp.dma_start(rawb[:, :], f_b1.rearrange("s m h -> s (m h)")).then_inc(loaded, 16)
                    sp.wait_ge(cleared, 2)
                    for s in range(S):
                        half = s // NQ
                        sp.dma_start(rawc[s * R:(s + 1) * R, :], f_c[s].rearrange("m r -> r m")).then_inc(loaded, 16)
                        sp.dma_start(w2[:, s, :, half * R:(half + 1) * R],
                                     f_w2[s].rearrange("m h r -> (m h) r").rearrange("(j p) r -> p j r", p=P))\
                          .then_inc(loaded, 16)
                        for part in range(2):
                            sp.dma_start(rawb2[part * M:(part + 1) * M, s, half * R:(half + 1) * R], f_b2[s])\
                              .then_inc(loaded, 16)
                        q = s % NQ
                        row = 2 * R * q + R * half
                        sp.dma_start(g1[row:row + R, :], f_g1[s * R:(s + 1) * R, :]).then_inc(loaded, 16)
                        sp.dma_start(pm_hi[:, s * R:(s + 1) * R], f_p[s, 0:P, :]).then_inc(loaded, 16)
                        sp.dma_start(pm_lo[:, s * R:(s + 1) * R], f_p[s, P:D, :]).then_inc(loaded, 16)
                    sp.dma_start(g1b[:, :], f_g1b.rearrange("(g a) -> g a", a=1)).then_inc(loaded, 16)
                    sp.dma_start(g2[:, :], f_g2).then_inc(loaded, 16)
                    sp.dma_start(g2b_bc[:, :], f_g2b.rearrange("(a d) -> a d", a=1).to_broadcast([P, D]))\
                      .then_inc(loaded, 16)
                    n_loads = S + 1 + 7 * S + 3
                    sp.wait_ge(loaded, 16 * n_loads)
                    sp.wait_ge(split, 3)
                    for s in range(S):
                        rows = slice(s * R, (s + 1) * R)
                        q, base = s % NQ, HALF * (s // NQ)
                        for g, part in enumerate(WPART):
                            to = slice(base + g * R, base + (g + 1) * R)
                            sp.dma_start(w1[to, q, :].bitcast(F32), raw1p[rows, part, :].bitcast(F32)).then_inc(placed, 16)
                            sp.dma_start(cm[to, q, :].bitcast(F32), rawcp[rows, part, :].bitcast(F32)).then_inc(placed, 16)
                        for g in range(2):
                            to = base + ZR + g
                            sp.dma_start(w1[to:to + 1, q, :].bitcast(F32), rawbp[s:s + 1, g, :].bitcast(F32)).then_inc(placed, 16)
                    sp.wait_ge(placed, 16 * 8 * S)


            @block.vector
            def _(dve):
                n_loads = S + 1 + 7 * S + 3
                for base in (0, HALF):
                    dve.memset(zst[base + 32:base + HALF, :, :].bitcast(F32), 1.0)
                dve.wait_ge(loaded, 16 * n_loads)
                for raw, parts in ((raw1[:, :], raw1p), (rawb[:, :], rawbp), (rawc[:, :], rawcp)):
                    dve.tensor_copy(parts[:, 0, :], raw).then_inc(step, 1)
                dve.wait_ge(step, 3)
                for raw, parts in ((raw1[:, :], raw1p), (rawb[:, :], rawbp), (rawc[:, :], rawcp)):
                    dve.tensor_tensor(parts[:, 1, :], raw, parts[:, 0, :].bitcast(F32), ALU.subtract).then_inc(split, 1)
                n = [3]

                def link(ins):
                    n[0] += 1
                    ins.then_inc(step, 1)
                    dve.wait_ge(step, n[0])

                link(dve.tensor_copy(b2[:, 0], rawb2[:, :, :]))
                link(dve.tensor_tensor(rawb2r[:, :, :], rawb2[:, :, :], b2[:, 0], ALU.subtract))
                link(dve.tensor_copy(b2[:, 1], rawb2r[:, :, :]))
                link(dve.tensor_tensor(rawb2r[:, :, :], rawb2r[:, :, :], b2[:, 1], ALU.subtract))
                dve.tensor_copy(b2[:, 2], rawb2r[:, :, :])

        SETUP_STEPS = 8
        c = sb("ln_c", [P, GW])
        xn = sb("ln_xn", [P, GW])
        sq = sb("ln_sq", [P, GW])
        small = sb("ln_small", [P, 4 * GT])
        xt_hi, xt_lo = sb("x2t_hi", [P, GTOK]), sb("x2t_lo", [DLO, GTOK])
        zp = sb("zp", [P, 2, GTOK], F32R)
        sc = sb("sc", [P, GT * S, TOP])
        scr = sb("scr", [P, GT * S, TOP])
        top = sb("top", [P, GT * S, 8])
        holder = sb("holder", [P, 1])
        den = sb("den", [P, GT * S, TOPK])
        rden = sb("rden", [P, 2, GT * S])
        ew = sb("ew", [P, GT * S, M])
        wsp = sb("wsp", [P, GT * S, 2, M], F16)
        wT = sb("wT", [P, S, GTOK], F16)
        hid = sb("hid", [P, 2, NQ, GTOK])
        hw = sb("hw", [P, 2, NQ, GTOK])
        comb = sb("comb", [P, GTOK])
        gh = sb("gh", [GH, GTOK])

        block = own.enter_context(nc.Block())

        @block.sync
        def _(sp):
            sp.sem_inc(out_stored, 16)
            with sp.Fori(0, NG) as g:
                sp.wait_ge(z_split, g + 1)
                sp.dma_start(z_dram.rearrange("a p n -> p a n"), zp[:, :, :].bitcast(F32)).then_inc(z_stored, 16)
                sp.wait_ge(z_stored, g * 16 + 16)
                for base, s0 in ((0, 0), (HALF, NQ)):
                    for k, part in enumerate(ZPART):
                        sp.dma_start(zst[base + k * R:base + (k + 1) * R, :, :].bitcast(F32),
                                     z_dram[part, s0 * R:(s0 + NQ) * R, :].rearrange("(s r) n -> r s n", r=R))\
                          .then_inc(z_in, 16)
                sp.wait_ge(out_ready, g + 1)
                sp.dma_start(out[bass.ds(g * GTOK, GTOK), :].rearrange("(c p) d -> p c d", p=P),
                             c[:, :].rearrange("p (c d) -> p c d", d=D)).then_inc(out_stored, 16)
            sp.wait_ge(out_stored, NG * 16 + 16)

        @block.tensor
        def _(pe):
            with pe.Fori(0, NG) as g:
                pe.wait_ge(xn_ready, g + 1)
                for t in range(GT):
                    pe.transpose(psum[0][:, t * P:(t + 1) * P], xn[:, t * D:t * D + P], ident[:, :])
                    last = pe.transpose(psum[1][0:DLO, t * P:(t + 1) * P], xn[:, t * D + P:(t + 1) * D], ident[:, :])
                last.then_inc(x_turned, 1)
                pe.wait_ge(x_copied, g + 1)
                pe.matmul(psum[2], pm_hi[:, :], xt_hi[:, :], start=True, stop=False)
                pe.matmul(psum[2], pm_lo[:, :], xt_lo[:, :], start=False, stop=True).then_inc(z_done, 1)
                pe.wait_ge(z_in, g * 96 + 96)
                for k in range(4):
                    half, t2 = divmod(k, 2)
                    rows = slice(HALF * half, HALF * half + ZR)
                    for t in (2 * t2, 2 * t2 + 1):
                        for q in range(NQ):
                            o = ((t % 2) * NQ + q) * M
                            last = pe.matmul(psum[k][:, o:o + M], zst[rows, q, t * P:(t + 1) * P],
                                             cm[rows, q, :], start=True, stop=True)
                    last.then_inc(scored, 1)
                pe.wait_ge(w_ready, g + 1)
                for s in range(S):
                    dst = psum[4 + s // 2].bitcast(F16)
                    for t in range(GT):
                        o = (s % 2) * GTOK + t * P
                        last = pe.transpose(dst[:, o:o + P], wsp[:, t * S + s, :, :].rearrange("p a m -> p (a m)"),
                                            ident16[:, :])
                    if s % 2:
                        last.then_inc(w_turned, 1)
                pe.wait_ge(w_copied, g * 4 + 4)
                for s in range(S):
                    q, half = s % NQ, s // NQ
                    for part in range(3):
                        pe.matmul(psum[7][32 * q:32 * q + 32, :], b2[:, part, s, :], wT[:, s, :],
                                  start=(half == 0 and part == 0), stop=False)

                def up(n):
                    half, j = divmod(n, NJ)
                    if n:
                        pe.wait_ge(gelu_done, g * (2 * NSTEP) + 2 * n)
                    rows = slice(HALF * half, HALF * half + KR)
                    for q in range(NQ):
                        last = pe.matmul(psum[q], w1[rows, q, j * P:(j + 1) * P], zst[rows, q, :],
                                         start=True, stop=True)
                        if q % 2:
                            last.then_inc(up_done, 1)

                def spread_weights(n):
                    half, j = divmod(n, NJ)
                    for q in range(NQ):
                        k = NQ * n + q
                        if k >= WBANKS:
                            pe.wait_ge(mixed, g * (NQ * NSTEP) + k - WBANKS + 1)
                        pe.matmul(psum[4 + k % WBANKS], select[:, j, :], wT[:, q + NQ * half, :],
                                  start=True, stop=True).then_inc(spread, 1)

                def down(n):
                    half, j = divmod(n, NJ)
                    for q in range(NQ):
                        if q == 0 or q == 1:
                            pe.wait_ge(mixed, g * (NQ * NSTEP) + NQ * n + (1, NQ)[q])
                        last = pe.matmul(psum[7][32 * q:32 * q + 32, :], w2[:, q + NQ * half, j, :], hw[:, n % 2, q, :],
                                         start=False, stop=(n == NSTEP - 1))
                    last.then_inc(down_done, 1)

                up(0)
                for n in range(NSTEP):
                    spread_weights(n)
                    if n:
                        down(n - 1)
                    if n + 1 < NSTEP:
                        up(n + 1)
                down(NSTEP - 1)
                pe.wait_ge(comb_ready, g + 1)
                pe.matmul(psum[0][0:GH, :], g1[:, :], comb[:, :], start=True, stop=True).then_inc(g1_done, 1)
                pe.wait_ge(gh_ready, g + 1)
                for t in range(GT):
                    last = pe.matmul(psum[1 + t // 2][:, (t % 2) * 256:(t % 2) * 256 + D], gh[:, t * P:(t + 1) * P],
                                     g2[:, :], start=True, stop=True)
                last.then_inc(g2_done, 1)

        @block.scalar
        def _(act):
            with act.Fori(0, NG) as g:
                act.wait_ge(lnvar, g + 1)
                act.activation(small[:, 2 * GT:3 * GT], small[:, GT:2 * GT], ACT.Sqrt).then_inc(lnstd, 1)
                act.wait_ge(x_turned, g + 1)
                act.activation(xt_hi[:, :], psum[0], ACT.Copy)
                act.activation(xt_lo[:, :], psum[1][0:DLO, :], ACT.Copy).then_inc(x_copied, 1)
                act.wait_ge(z_done, g + 1)
                act.activation(zp[:, 0, :], psum[2], ACT.Copy).then_inc(zh_done, 1)
                for k in range(4):
                    half, t2 = divmod(k, 2)
                    act.wait_ge(scored, g * 4 + k + 1)
                    for t in range(2):
                        o = (2 * t2 + t) * S + half * NQ
                        last = act.activation(sc[:, o:o + NQ, 0:M],
                                              psum[k][:, t * 256:(t + 1) * 256].rearrange("p (q m) -> p q m", m=M),
                                              ACT.Copy)
                    last.then_inc(sc_copied, 1)
                act.wait_ge(exp_asked, g + 1)
                act.activation(den[:, :, :], den[:, :, :], ACT.Exp)
                act.activation(ew[:, :, :], ew[:, :, :], ACT.Exp).then_inc(exp_done, 1)
                for k in range(4):
                    act.wait_ge(w_turned, g * 4 + k + 1)
                    act.activation(wT[:, 2 * k:2 * k + 2, :],
                                   psum[4 + k].bitcast(F16).rearrange("p (s n) -> p s n", n=GTOK),
                                   ACT.Copy).then_inc(w_copied, 1)
                for n in range(NSTEP):
                    if n >= 2:
                        act.wait_ge(mixed, g * (NQ * NSTEP) + NQ * (n - 1))
                    for pair in range(2):
                        act.wait_ge(up_done, g * (2 * NSTEP) + 2 * n + pair + 1)
                        act.activation(hid[:, n % 2, 2 * pair:2 * pair + 2, :],
                                       banks[:, pair * 1024:(pair + 1) * 1024].rearrange("p (q n) -> p q n", n=GTOK),
                                       ACT.Gelu_apprx_tanh).then_inc(gelu_done, 1)
                act.wait_ge(g1_done, g + 1)
                act.activation(gh[:, :], psum[0][0:GH, :], ACT.Gelu_apprx_tanh, bias=g1b[:, 0:1]).then_inc(gh_ready, 1)

        @block.vector
        def _(dve):
            dve.memset(sc[:, :, M:TOP], BIG).then_inc(step, 1)
            dve.wait_ge(step, SETUP_STEPS)
            with dve.Fori(0, NG) as g:
                n = [0]

                def link(ins):
                    n[0] += 1
                    ins.then_inc(step, 1)
                    dve.wait_ge(step, g * STEPS + n[0] + SETUP_STEPS)

                tok = lambda a: a.rearrange("p (n d) -> p n d", d=D)
                dve.wait_ge(out_stored, g * 16 + 16)
                link(dve.tensor_scalar(xn[:, :], h_all[:, bass.ds(g * GW, GW)], 1.0, None, ALU.mult))
                normalise_chain(dve, link, tok(xn[:, :]), tok(c[:, :]), tok(sq[:, :]), small, lnvar, lnstd,
                                g + 1, g + 1)
                dve.tensor_tensor(tok(xn[:, :]), tok(c[:, :]),
                                  small[:, 2 * GT:3 * GT].unsqueeze(2).to_broadcast([P, GT, D]),
                                  ALU.mult).then_inc(xn_ready, 1)
                dve.wait_ge(zh_done, g + 1)
                dve.tensor_tensor(zp[:, 1, :], psum[2], zp[:, 0, :].bitcast(F32), ALU.subtract).then_inc(z_split, 1)
                dve.wait_ge(sc_copied, g * GT + GT)
                dve.memset(holder[:, :], 0.0)
                for k in range(GT * S):
                    last = dve.max(top[:, k, :], sc[:, k, :])
                link(last)
                best = lambda w: top[:, :, TOPK:TOPK + 1].to_broadcast([P, GT * S, w])
                dve.tensor_tensor(den[:, :, :], top[:, :, TOPK:2 * TOPK], best(TOPK), ALU.subtract)
                dve.tensor_tensor(ew[:, :, :], sc[:, :, 0:M], best(M), ALU.subtract).then_inc(exp_asked, 1)
                for k in range(GT * S):
                    last = dve.match_replace(scr[:, k, :], top[:, k, :], sc[:, k, :], TAKEN)
                link(last)
                dve.wait_ge(exp_done, g + 1)
                link(dve.tensor_reduce(rden[:, 0, :], den[:, :, :], AX.X, ALU.add))
                link(dve.reciprocal(rden[:, 1, :], rden[:, 0, :]))
                link(dve.scalar_tensor_tensor(ew[:, :, :], scr[:, :, 0:M], TAKEN, ew[:, :, :], ALU.is_equal, ALU.mult))
                link(dve.tensor_tensor(ew[:, :, :], ew[:, :, :],
                                       rden[:, 1, :].unsqueeze(2).to_broadcast([P, GT * S, M]), ALU.mult))
                link(dve.tensor_copy(wsp[:, :, 0, :], ew[:, :, :]))
                dve.tensor_tensor(wsp[:, :, 1, :], ew[:, :, :], wsp[:, :, 0, :], ALU.subtract).then_inc(w_ready, 1)
                for m in range(NSTEP):
                    if m >= 2:
                        dve.wait_ge(down_done, g * NSTEP + m - 1)
                    for q in range(NQ):
                        k = NQ * m + q
                        dve.wait_ge(gelu_done, g * (2 * NSTEP) + 2 * m + q // 2 + 1)
                        dve.wait_ge(spread, g * (NQ * NSTEP) + k + 1)
                        dve.tensor_tensor(hw[:, m % 2, q, :], hid[:, m % 2, q, :], psum[4 + k % WBANKS],
                                          ALU.mult).then_inc(mixed, 1)
                dve.wait_ge(down_done, g * NSTEP + NSTEP)
                dve.tensor_copy(comb[:, :], psum[7]).then_inc(comb_ready, 1)
                dve.wait_ge(g2_done, g + 1)
                for t in range(GT):
                    last = dve.tensor_tensor(c[:, t * D:(t + 1) * D],
                                             psum[1 + t // 2][:, (t % 2) * 256:(t % 2) * 256 + D], g2b_bc[:, :], ALU.add)
                link(last)
                dve.tensor_tensor(c[:, :], c[:, :], h_all[:, bass.ds(g * GW, GW)], ALU.add).then_inc(out_ready, 1)
                assert n[0] == STEPS, n


_INS = ['x', 'L0_tok_weight', 'L0_attn_W_Q', 'L0_attn_b_Q', 'L0_attn_W_K', 'L0_attn_b_K', 'L0_attn_W_V',
        'L0_attn_b_V', 'L0_attn_W_O', 'L0_attn_b_O', 'L0_ffn_P', 'L0_ffn_C', 'L0_ffn_W1', 'L0_ffn_b1',
        'L0_ffn_W2', 'L0_ffn_b2', 'L0_ffn_G1', 'L0_ffn_g1b', 'L0_ffn_G2', 'L0_ffn_g2b']
STAGES = 3


def kernel(**inputs):
    import numpy as np
    import concourse.bacc as bacc
    from concourse.bass_utils import run_bass_kernel_spmd

    nc = bacc.Bacc("TRN2", target_bir_lowering=False, num_devices=1)
    arrays, args = {}, []
    for name in _INS:
        a = np.ascontiguousarray(inputs[name])
        if name == 'x':
            a = np.ascontiguousarray(a.reshape(NT, P).T)
        arrays[f"in_{name}"] = a
        args.append(nc.dram_tensor(f"in_{name}", a.shape, mybir.dt.from_np(a.dtype), kind="ExternalInput").ap())
    o = nc.dram_tensor("out_h", (B * T, D), F32, kind="ExternalOutput").ap()
    tower(nc, *args, o, stages=STAGES)
    r = run_bass_kernel_spmd(nc, [arrays], core_ids=[0])
    return r.results[0]["out_h"].reshape(B, T, D)
```

```python
import concourse.bass as bass
from concourse import mybir
from contextlib import ExitStack

F32 = mybir.dt.float32
F32R = mybir.dt.float32r
F16 = mybir.dt.float16
BF16 = mybir.dt.bfloat16
I32 = mybir.dt.int32
ALU = mybir.AluOpType
ACT = mybir.ActivationFunctionType
AX = mybir.AxisListType

P = 128
B, T, D = 2, 2048, 192
DLO = D - P
NT = B * T // P
GT = 4
NG = NT // GT
GW = GT * D
GTOK = GT * P
H, E = 12, 64
NP = H // 2
KT = T // P
S, R, M, HID = 8, 16, 64, 32
NJ = M * HID // P
NQ = 4
GH = 64
TOPK = 4
VOCAB = 50257

QB = 64
NB = GW // QB
QEPS = 1e-12
LNEPS = 1e-5
ROUND = 12582912.0
NEG = -3.0e38
MASKED = -1.0e30
NF4 = [-1.0, -0.6961928009986877, -0.5250730514526367, -0.39491748809814453, -0.28444138169288635,
       -0.18477343022823334, -0.09105003625154495, 0.0, 0.07958029955625534, 0.16093020141124725,
       0.24611230194568634, 0.33791524171829224, 0.44070982933044434, 0.5626170039176941,
       0.8481764793395996, 1.0]


def nf4_midpoints():
    import numpy as np
    v = np.array(NF4, np.float32)
    return [float(x) for x in (v[1:] + v[:-1]) * np.float32(0.5)]


MID = nf4_midpoints()
STEP = [NF4[i + 1] - NF4[i] for i in range(15)]


def tower(nc, x, tok_w, w_q, b_q, w_k, b_k, w_v, b_v, w_o, b_o,
          f_p, f_c, f_w1, f_b1, f_w2, f_b2, f_g1, f_g1b, f_g2, f_g2b, out, stages=3):
    ctx = ExitStack()
    with ctx:
        def sb(name, shape, dt=F32):
            return ctx.enter_context(nc.sbuf_tensor(name, shape, dt))

        xT_dram = nc.dram_tensor("xT_scratch", (D, B * T), F32, kind="Internal").ap()

        h_all = sb("h_all", [P, NT * D])
        ident = sb("ident", [P, P])
        idx = sb("idx", [P, NT], I32)
        bo_bc = sb("bo_bc", [P, D])
        banks = ctx.enter_context(nc.psum_tensor("banks", [P, 8 * 512], F32))
        psum = [banks[:, i * 512:(i + 1) * 512] for i in range(8)]

        stage_embed(nc, x, tok_w, b_o, h_all, ident, idx, bo_bc, psum, xT_dram)
        if stages >= 2:
            stage_attention(nc, w_q, b_q, w_k, b_k, w_v, b_v, w_o, h_all, ident, psum, xT_dram)
        if stages >= 3:
            stage_experts(nc, f_p, f_c, f_w1, f_b1, f_w2, f_b2, f_g1, f_g1b, f_g2, f_g2b,
                          h_all, ident, banks, psum, out)
        else:
            with nc.semaphore("dbg") as dbg, nc.Block() as block:
                @block.sync
                def _(sp):
                    sp.dma_start(out.rearrange("(n p) d -> p n d", p=P),
                                 h_all[:, :].rearrange("p (n d) -> p n d", d=D)).then_inc(dbg, 16)
                    sp.wait_ge(dbg, 16)


def normalise_chain(dve, link, src, c, sq, small, sqrt_asked, sqrt_done, asked, done):
    mean, var, rstd, t = (small[:, GT * i:GT * i + GT] for i in range(4))
    wide = lambda a: a.unsqueeze(2).to_broadcast([P, GT, D])
    link(dve.tensor_reduce(mean, src, AX.X, ALU.add))
    link(dve.tensor_scalar(mean, mean, 1.0 / D, None, ALU.mult))
    link(dve.tensor_tensor(c, src, wide(mean), ALU.subtract))
    link(dve.tensor_tensor(sq, c, c, ALU.mult))
    link(dve.tensor_reduce(var, sq, AX.X, ALU.add))
    dve.tensor_scalar(var, var, 1.0 / D, LNEPS, ALU.mult, ALU.add).then_inc(sqrt_asked, 1)
    dve.wait_ge(sqrt_done, done)
    link(dve.reciprocal(rstd, rstd))
    link(dve.tensor_tensor(t, rstd, rstd, ALU.mult))
    link(dve.tensor_tensor(t, t, var, ALU.mult))
    link(dve.tensor_scalar(t, t, -0.5, 1.5, ALU.mult, ALU.add))
    link(dve.tensor_tensor(rstd, rstd, t, ALU.mult))


def stage_embed(nc, x, tok_w, b_o, h_all, ident, idx, bo_bc, psum, xT_dram):
    with ExitStack() as own:
        def sb(name, shape, dt=F32):
            return own.enter_context(nc.sbuf_tensor(name, shape, dt))

        def sem(name):
            return own.enter_context(nc.semaphore(name))

        raw = sb("raw", [P, NT * D])
        xg = sb("xg", [P, GW])
        main = sb("main", [P, GW])
        work = sb("work", [P, GW])
        res = sb("res", [P, GW])
        gate = sb("gate", [P, GW])
        level = sb("level", [P, GW])
        xn = sb("xn", [P, GW])
        xs_hi = sb("xs_hi", [P, GTOK])
        xs_lo = sb("xs_lo", [DLO, GTOK])
        blk = sb("blk", [P, 8 * NB])
        small = sb("small", [P, 4 * GT])

        idx_in, bias_in = sem("idx_in"), sem("bias_in")
        first_rows_in, rows_in = sem("first_rows_in"), sem("rows_in")
        const_ready = sem("const_ready")
        step = sem("embed_step")
        qvar_ready, qstd_ready = sem("qvar_ready"), sem("qstd_ready")
        lnvar_ready, lnstd_ready = sem("lnvar_ready"), sem("lnstd_ready")
        xn_ready, xT_turned, xT_copied, xT_stored = (sem("xn_ready"), sem("xT_turned"),
                                                     sem("xT_copied"), sem("xT_stored"))
        STEPS = 69

        block = own.enter_context(nc.Block())

        @block.sync
        def _(sp):
            sp.sem_inc(xT_stored, 32)
            sp.dma_start(idx[:, :], x).then_inc(idx_in, 16)
            sp.dma_start(bo_bc[:, :], b_o.rearrange("(a d) -> a d", a=1).to_broadcast([P, D])).then_inc(bias_in, 16)
            with sp.Fori(0, NG) as g:
                sp.wait_ge(xT_copied, g + 2)
                sp.dma_start(xT_dram[0:P, bass.ds(g * GTOK, GTOK)], xs_hi[:, :]).then_inc(xT_stored, 16)
                sp.dma_start(xT_dram[P:D, bass.ds(g * GTOK, GTOK)], xs_lo[:, :]).then_inc(xT_stored, 16)
            sp.wait_ge(xT_stored, 32 * NG + 32)

        @block.gpsimd
        def _(pool):
            pool.memset(ident[:, :], 0.0).then_inc(const_ready, 1)
            pool.wait_ge(const_ready, 1)
            pool.affine_select(out=ident[:, :], in_=ident[:, :], pattern=[[-1, P]], compare_op=ALU.not_equal,
                               fill=1.0, base=0, channel_multiplier=1).then_inc(const_ready, 1)
            pool.wait_ge(idx_in, 16)
            for n in range(NT):
                pool.indirect_dma_start(out=raw[:, n * D:(n + 1) * D], out_offset=None, in_=tok_w,
                                        in_offset=bass.IndirectOffsetOnAxis(ap=idx[:, n:n + 1], axis=0),
                                        bounds_check=VOCAB - 1, oob_is_err=False)\
                    .then_inc(first_rows_in if n < GT else rows_in, 16)

        @block.vector
        def _(dve):
            dve.wait_ge(bias_in, 16)
            blocks = lambda a: a.rearrange("p (n q) -> p n q", q=QB)
            wide = lambda a: a.unsqueeze(2).to_broadcast([P, NB, QB])
            amax, var, s, r, t, scale, s127, rmax = (blk[:, NB * i:NB * i + NB] for i in range(8))

            def group(g):
                n = [0]

                def link(ins):
                    n[0] += 1
                    ins.then_inc(step, 1)
                    dve.wait_ge(step, g * STEPS + n[0])

                X = xg[:, :]
                link(dve.tensor_scalar(X, raw[:, bass.ds(g * GW, GW)], 1.0, None, ALU.mult))
                Xb, Wb, Mb, Rb, Gb, Lb = map(blocks, (X, work[:, :], main[:, :], res[:, :], gate[:, :], level[:, :]))
                link(dve.tensor_reduce(amax, Xb, AX.X, ALU.max, apply_absolute_value=True))
                link(dve.tensor_reduce(s, Xb, AX.X, ALU.add))
                link(dve.tensor_scalar(s, s, 1.0 / QB, None, ALU.mult))
                link(dve.tensor_tensor(Wb, Xb, wide(s), ALU.subtract))
                link(dve.tensor_tensor(Wb, Wb, Wb, ALU.mult))
                link(dve.tensor_reduce(var, Wb, AX.X, ALU.add))
                dve.tensor_scalar(var, var, 1.0 / QB, None, ALU.mult).then_inc(qvar_ready, 1)
                dve.wait_ge(qstd_ready, g + 1)
                link(dve.tensor_scalar(s, s, 1e-18, None, ALU.max))
                link(dve.reciprocal(r, s))
                link(dve.tensor_tensor(r, r, var, ALU.mult))
                link(dve.tensor_tensor(s, s, r, ALU.add))
                link(dve.tensor_scalar(s, s, 1.5, None, ALU.mult))
                link(dve.tensor_tensor(s, s, amax, ALU.min))
                link(dve.tensor_scalar(scale, s, QEPS, None, ALU.max))
                link(dve.reciprocal(r, scale))
                link(dve.tensor_scalar(s127, scale, 1.0 / 127.0, None, ALU.mult))
                link(dve.tensor_tensor(Wb, Xb, wide(r), ALU.mult))
                link(dve.tensor_scalar(work[:, :], work[:, :], 127.0, ROUND, ALU.mult, ALU.add))
                link(dve.tensor_scalar(work[:, :], work[:, :], ROUND, 127.0, ALU.subtract, ALU.min))
                link(dve.scalar_tensor_tensor(Mb, Wb, -127.0, wide(s127), ALU.max, ALU.mult))
                link(dve.tensor_tensor(res[:, :], X, main[:, :], ALU.subtract))
                link(dve.tensor_reduce(rmax, Rb, AX.X, ALU.max, apply_absolute_value=True))
                link(dve.tensor_scalar(rmax, rmax, QEPS, None, ALU.max))
                link(dve.reciprocal(t, rmax))
                link(dve.tensor_tensor(Rb, Rb, wide(t), ALU.mult))
                link(dve.tensor_scalar(level[:, :], res[:, :], MID[14], STEP[14], ALU.is_gt, ALU.mult))
                for j in range(13, -1, -1):
                    g_j = (gate, work)[j % 2]
                    link(dve.tensor_scalar(g_j[:, :], res[:, :], MID[j], None, ALU.is_gt))
                    link(dve.scalar_tensor_tensor(level[:, :], level[:, :], STEP[j], g_j[:, :], ALU.add, ALU.mult))
                link(dve.scalar_tensor_tensor(Lb, Lb, NF4[0], wide(rmax), ALU.add, ALU.mult))
                link(dve.tensor_tensor(level[:, :], level[:, :], main[:, :], ALU.add))
                link(dve.tensor_tensor(level[:, :], level[:, :], X, ALU.subtract))
                link(dve.tensor_tensor(level[:, :], level[:, :], X, ALU.add))
                tok = lambda a: a.rearrange("p (n d) -> p n d", d=D)
                link(dve.tensor_tensor(tok(h_all[:, bass.ds(g * GW, GW)]), tok(level[:, :]),
                                       bo_bc[:, :].unsqueeze(1).to_broadcast([P, GT, D]), ALU.add))
                normalise_chain(dve, link, tok(level[:, :]), tok(work[:, :]), tok(main[:, :]), small,
                                lnvar_ready, lnstd_ready, g + 1, g + 1)
                dve.wait_ge(xT_turned, g + 1)
                dve.tensor_tensor(tok(xn[:, :]), tok(work[:, :]),
                                  small[:, 2 * GT:3 * GT].unsqueeze(2).to_broadcast([P, GT, D]),
                                  ALU.mult).then_inc(xn_ready, 1)
                assert n[0] == STEPS
                dve.wait_ge(xn_ready, g + 1)

            dve.wait_ge(first_rows_in, 16 * GT)
            group(0)
            dve.wait_ge(rows_in, 16 * (NT - GT))
            with dve.Fori(1, NG) as g:
                group(g)

        @block.scalar
        def _(act):
            act.sem_inc(xT_copied, 1)
            with act.Fori(0, NG) as g:
                act.wait_ge(qvar_ready, g + 1)
                act.activation(blk[:, 2 * NB:3 * NB], blk[:, NB:2 * NB], ACT.Sqrt).then_inc(qstd_ready, 1)
                act.wait_ge(lnvar_ready, g + 1)
                act.activation(small[:, 2 * GT:3 * GT], small[:, GT:2 * GT], ACT.Sqrt).then_inc(lnstd_ready, 1)
                act.wait_ge(xT_turned, g + 2)
                act.wait_ge(xT_stored, 32 * g + 32)
                act.activation(xs_hi[:, :], psum[0][:, :], ACT.Copy)
                act.activation(xs_lo[:, :], psum[1][0:DLO, :], ACT.Copy).then_inc(xT_copied, 1)

        @block.tensor
        def _(pe):
            pe.sem_inc(xT_turned, 1)
            pe.wait_ge(const_ready, 2)
            with pe.Fori(0, NG) as g:
                pe.wait_ge(xn_ready, g + 1)
                pe.wait_ge(xT_copied, g + 1)
                for c in range(GT):
                    pe.transpose(psum[0][:, c * P:(c + 1) * P], xn[:, c * D:c * D + P], ident[:, :])
                    last = pe.transpose(psum[1][0:DLO, c * P:(c + 1) * P], xn[:, c * D + P:(c + 1) * D], ident[:, :])
                last.then_inc(xT_turned, 1)


def stage_attention(nc, w_q, b_q, w_k, b_k, w_v, b_v, w_o, h_all, ident, psum, xT_dram):
    CH = 512
    PC = CH // P
    CHUNKS = [i // PC + 1 for i in range(KT)]
    NC = sum(CHUNKS)
    BEFORE = [sum(CHUNKS[:i]) for i in range(KT)]
    ITEMS = 6 + NC + KT
    SLOTS = 3
    LSLOTS = 8
    STEPS = 2 * KT
    with ExitStack() as own:
        def sb(name, shape, dt=F32):
            return own.enter_context(nc.sbuf_tensor(name, shape, dt))

        def sem(name):
            return own.enter_context(nc.semaphore(name))

        xt_hi = sb("xt_hi", [P, T])
        xt_lo = sb("xt_lo", [P, T // 2])
        w_hi = sb("w_hi", [P, 3, P])
        w_lo = sb("w_lo", [P, 3, P])
        wo = sb("wo", [P, D])
        bq, bk, bv_bc = sb("bq", [P, 1]), sb("bk", [P, 1]), sb("bv_bc", [P, P])
        q_hi, q_lo = sb("q_hi", [P, 2, T], F32R), sb("q_lo", [P, 2, T], F32R)
        k_parts, v = sb("k_parts", [P, 2, T], F32R), sb("v", [P, KT, P])
        probs = sb("probs", [P, SLOTS, 2, T])
        probsT = sb("probsT", [P, 2, 2, KT, P])
        oT = sb("oT", [P, 2, P])
        mask = sb("mask", [P, P])
        part = sb("part", [P, 2, KT // PC + 1])
        negmax = sb("negmax", [P, SLOTS, 2])
        total = sb("total", [P, LSLOTS, 2])
        rtotal = sb("rtotal", [P, LSLOTS, 2])

        mask_ready = sem("mask_ready")
        x_in, w_in, wo_in = sem("x_in"), sem("w_in"), sem("wo_in")
        projected, hi_done = sem("projected"), sem("hi_done")
        filled, emptied = sem("ring_filled"), sem("ring_emptied")
        max_ready, exp_done = sem("max_ready"), sem("exp_done")
        turned = [sem("turned_a"), sem("turned_b")]
        copied = [sem("copied_a"), sem("copied_b")]
        weighed, oT_copied = sem("weighed"), sem("oT_copied")
        step = sem("attn_step")

        pairs = [("q", 0), ("v", 0), ("q", 1), ("v", 1), ("k", 0), ("k", 1)]
        order = list(pairs)
        for i in range(2):
            order += [("s", i, c) for c in range(CHUNKS[i])]
        for i in range(KT + 3):
            for c in range(KT // PC):
                if i + 2 < KT and c < CHUNKS[i + 2]:
                    order.append(("s", i + 2, c))
                if i >= 3 and c == 0:
                    order.append(("o", i - 3))
        assert len(order) == ITEMS and ITEMS % 2 == 0
        place = {item: n for n, item in enumerate(order)}

        def score_width(i, c):
            return min(CH, (i + 1) * P - c * CH)

        block = own.enter_context(nc.Block())

        @block.gpsimd
        def _(pool):
            pool.memset(mask[:, :], 0.0).then_inc(mask_ready, 1)
            pool.wait_ge(mask_ready, 1)
            pool.affine_select(out=mask[:, :], in_=mask[:, :], pattern=[[-1, P]], compare_op=ALU.is_ge,
                               fill=MASKED, base=0, channel_multiplier=1).then_inc(mask_ready, 1)

        @block.sync
        def _(sp):
            sp.sem_inc(projected, 1)
            with sp.Fori(0, B) as b:
                sp.wait_ge(projected, b * NP + 1)
                sp.dma_start(xt_hi[:, :], xT_dram[0:P, bass.ds(b * T, T)]).then_inc(x_in, 16)
                for half in range(2):
                    sp.dma_start(xt_lo[half * DLO:(half + 1) * DLO, :],
                                 xT_dram[P:D, bass.ds(b * T + half * (T // 2), T // 2)]).then_inc(x_in, 16)
                with sp.Fori(0, NP) as p:
                    it = b * NP + p
                    sp.wait_ge(projected, it + 1)
                    for n, w in enumerate((w_q, w_k, w_v)):
                        wd = w.rearrange("h d e -> d h e")
                        for dst, d0 in ((w_hi[:, n, :], 0), (w_lo[0:DLO, n, :], P), (w_lo[DLO:P, n, :], P)):
                            k = dst.shape[0]
                            sp.dma_start(dst.rearrange("d (h e) -> d h e", e=E),
                                         wd[d0:d0 + k, bass.ds(2 * p, 2), :]).then_inc(w_in, 16)
                    for dst, src in ((bq, b_q), (bk, b_k)):
                        sp.dma_start(dst[:, :], src.rearrange("h (e a) -> (h e) a", a=1)[bass.ds(p * P, P), :])\
                          .then_inc(w_in, 16)
                    sp.dma_start(bv_bc[:, :], b_v.rearrange("(a g) e -> a (g e)", g=2)[bass.ds(p, 1), :]
                                 .to_broadcast([P, P])).then_inc(w_in, 16)
                    sp.wait_ge(emptied, it * ITEMS + 2)
                    sp.dma_start(wo[:, :], w_o.rearrange("h e d -> (h e) d")[bass.ds(p * P, P), :])\
                      .then_inc(wo_in, 16)

        @block.tensor
        def _(pe):
            with pe.Fori(0, B) as b, pe.Fori(0, NP) as p:
                it = b * NP + p

                def slot_free(n):
                    pe.wait_ge(emptied, it * ITEMS + n + 1)
                    return psum[2 * (n % 2)], psum[2 * (n % 2) + 1]

                def project(kind, c):
                    n = place[(kind, c)]
                    banks = slot_free(n)
                    if kind == "v":
                        for h in range(2):
                            for k in range(PC):
                                t = (2 * h + c) * PC + k
                                pe.matmul(banks[h][:, k * P:(k + 1) * P], xt_hi[:, t * P:(t + 1) * P],
                                          w_hi[:, 2, :], start=(k == 0), stop=False, skip_group_check=True)
                        for k in range(PC):
                            for h in range(2):
                                t = c * PC + k
                                rows = slice(h * DLO, (h + 1) * DLO)
                                last = pe.matmul(banks[h][:, k * P:(k + 1) * P], xt_lo[rows, t * P:(t + 1) * P],
                                                 w_lo[rows, 2, :], start=False, stop=True, skip_group_check=True)
                    else:
                        w = "qk".index(kind)
                        for h in range(2):
                            t = (2 * h + c) * CH
                            pe.matmul(banks[h][:, :], w_hi[:, w, :], xt_hi[:, t:t + CH], start=True, stop=False)
                        for h in range(2):
                            rows = slice(h * DLO, (h + 1) * DLO)
                            last = pe.matmul(banks[h][:, :], w_lo[rows, w, :], xt_lo[rows, c * CH:(c + 1) * CH],
                                             start=False, stop=True)
                    last.then_inc(filled, 1)

                def score(i, c):
                    banks = slot_free(place[("s", i, c)])
                    w = score_width(i, c)
                    for h in range(2):
                        for q in (q_hi, q_lo):
                            last = pe.matmul(banks[h][:, 0:w], q[:, h, i * P:(i + 1) * P],
                                             k_parts[:, h, c * CH:c * CH + w], start=q is q_hi, stop=q is q_lo)
                    last.then_inc(filled, 1)

                def turn(i, c):
                    for h in range(2):
                        if c == 0:
                            pe.wait_ge(exp_done, it * 2 * KT + 2 * i + h + 1)
                        pe.wait_ge(copied[h], it * NC + BEFORE[i] + c + 1)
                        for k in range(c * PC, min(i + 1, (c + 1) * PC)):
                            last = pe.transpose(psum[4 + h][:, (k % PC) * P:(k % PC + 1) * P],
                                                probs[:, i % SLOTS, h, k * P:(k + 1) * P], ident[:, :])
                        last.then_inc(turned[h], 1)

                def weigh(i, c):
                    for h in range(2):
                        pe.wait_ge(copied[h], it * NC + BEFORE[i] + c + 2)
                    for k in range(c * PC, min(i + 1, (c + 1) * PC)):
                        for h in range(2):
                            rows = slice(h * E, (h + 1) * E)
                            last = pe.matmul(psum[6 + i % 2][rows, 0:P], v[:, k, rows], probsT[:, i % 2, h, k, :],
                                             start=(k == 0), stop=(k == i))
                    if (c + 1) * PC > i:
                        last.then_inc(weighed, 1)

                def output(i):
                    banks = slot_free(place[("o", i)])
                    if i == 0:
                        pe.wait_ge(wo_in, it * 16 + 16)
                    pe.wait_ge(oT_copied, it * KT + i + 1)
                    for h in range(2):
                        rows = slice(h * E, (h + 1) * E)
                        last = pe.matmul(banks[h][:, 0:D], oT[rows, i % 2, :], wo[rows, :], start=True, stop=True)
                    last.then_inc(filled, 1)

                pe.wait_ge(x_in, b * 48 + 48)
                pe.wait_ge(w_in, it * (12 * 16) + 12 * 16)
                for kind, c in pairs:
                    project(kind, c)
                for i in range(2):
                    for c in range(CHUNKS[i]):
                        score(i, c)
                for i in range(KT + 3):
                    for c in range(KT // PC):
                        if i < KT and c < CHUNKS[i]:
                            turn(i, c)
                        if i + 2 < KT and c < CHUNKS[i + 2]:
                            score(i + 2, c)
                        if 1 <= i <= KT and c < CHUNKS[i - 1]:
                            weigh(i - 1, c)
                        if i >= 3 and c == 0:
                            output(i - 3)

        @block.vector
        def _(dve):
            dve.wait_ge(mask_ready, 2)
            dve.sem_inc(max_ready, 1)
            dve.sem_inc(emptied, 2)
            dve.sem_inc(copied[1], 1)
            with dve.Fori(0, B) as b, dve.Fori(0, NP) as p:
                it = b * NP + p
                steps = [0]

                def link(ins):
                    steps[0] += 1
                    ins.then_inc(step, 1)
                    dve.wait_ge(step, it * STEPS + steps[0])

                def item(*key):
                    n = place[key]
                    dve.wait_ge(filled, it * ITEMS + n + 1)
                    return psum[2 * (n % 2)], psum[2 * (n % 2) + 1]

                def take_scores(i, c):
                    if c == 0:
                        dve.wait_ge(max_ready, it * KT + i + 1)
                    banks = item("s", i, c)
                    w = score_width(i, c)
                    diag = c == CHUNKS[i] - 1
                    whole = w - P if diag else w
                    if not whole:
                        dve.memset(part[:, :, c:c + 1], NEG)
                    for h in range(2):
                        dst = probs[:, i % SLOTS, h, c * CH:c * CH + w]
                        if whole:
                            last = dve.tensor_scalar(dst[:, 0:whole], banks[h][:, 0:whole], E ** -0.5, None, ALU.mult,
                                                     ALU.max, accum_out=part[:, h, c:c + 1])
                            if not diag and h == 1:
                                last.then_inc(emptied, 1)
                        if diag:
                            n = c + 1
                            last = dve.tensor_tensor_reduce(dst[:, whole:w], banks[h][:, whole:w], mask[:, :],
                                                            E ** -0.5, NEG, ALU.add, ALU.max, part[:, h, n:n + 1])
                            if h == 1:
                                last.then_inc(emptied, 1)
                    if diag:
                        dve.wait_ge(emptied, it * ITEMS + 2 + place[("s", i, c)] + 1)
                        dve.tensor_reduce(negmax[:, i % SLOTS, :], part[:, :, 0:n + 1], AX.X, ALU.max,
                                          negate=True).then_inc(max_ready, 1)

                def take_transposes(i, c):
                    dve.wait_ge(turned[1], it * NC + BEFORE[i] + c + 1)
                    a, z = c * PC, min(i + 1, (c + 1) * PC)
                    dve.tensor_copy(probsT[:, i % 2, 1, a:z, :],
                                    psum[5][:, 0:(z - a) * P].rearrange("p (k q) -> p k q", q=P))\
                       .then_inc(copied[1], 1)

                def take_output(i):
                    dve.wait_ge(exp_done, it * 2 * KT + 2 * i + 2)
                    link(dve.reciprocal(rtotal[:, i % LSLOTS, :], total[:, i % LSLOTS, :]))
                    banks = item("o", i)
                    h_tile = h_all[:, bass.ds(b * (KT * D) + i * D, D)]
                    link(dve.scalar_tensor_tensor(h_tile, banks[0][:, 0:D], rtotal[:, i % LSLOTS, 0:1], h_tile,
                                                  ALU.mult, ALU.add))
                    dve.scalar_tensor_tensor(h_tile, banks[1][:, 0:D], rtotal[:, i % LSLOTS, 1:2], h_tile,
                                             ALU.mult, ALU.add).then_inc(emptied, 1)

                dve.wait_ge(w_in, it * (12 * 16) + 12 * 16)
                def take_low(kind, c, nth):
                    banks = item(kind, c)
                    for half in range(2):
                        dve.wait_ge(hi_done, it * 8 + nth * 2 + half + 1)
                        t = slice((2 * half + c) * CH, (2 * half + c + 1) * CH)
                        for h in range(2):
                            own, other = (slice(j * E, (j + 1) * E) for j in (h, 1 - h))
                            hi, lo, bias = (k_parts, k_parts, bk) if kind == "k" else (q_hi, q_lo, bq)
                            for to in (other,) if kind == "k" else (own, other):
                                last = dve.scalar_tensor_tensor(lo[to, h, t], banks[half][own, :], bias[own, 0:1],
                                                                hi[own, h, t].bitcast(F32), ALU.add, ALU.subtract)
                    last.then_inc(emptied, 1)

                def take_v(c):
                    banks = item("v", c)
                    for h in range(2):
                        t = (2 * h + c) * PC
                        last = dve.tensor_tensor(v[:, t:t + PC, :], banks[h][:, :].rearrange("p (k e) -> p k e", e=P),
                                                 bv_bc[:, :].unsqueeze(1).to_broadcast([P, PC, P]), ALU.add)
                    last.then_inc(emptied, 1)

                for c in range(2):
                    take_low("q", c, c)
                    take_v(c)
                for c in range(2):
                    take_low("k", c, 2 + c)
                dve.wait_ge(emptied, it * ITEMS + 2 + 6)
                dve.sem_inc(projected, 1)
                for i in range(2):
                    for c in range(CHUNKS[i]):
                        take_scores(i, c)
                for i in range(KT + 3):
                    for c in range(KT // PC):
                        if i < KT and c < CHUNKS[i]:
                            take_transposes(i, c)
                        if i + 2 < KT and c < CHUNKS[i + 2]:
                            take_scores(i + 2, c)
                        if i >= 3 and c == 0:
                            take_output(i - 3)
                assert steps[0] == STEPS, steps

        @block.scalar
        def _(act):
            act.sem_inc(copied[0], 1)
            with act.Fori(0, B) as b, act.Fori(0, NP) as p:
                it = b * NP + p

                def exponentials(i, h):
                    act.wait_ge(max_ready, it * KT + i + 2)
                    row = probs[:, i % SLOTS, h, 0:(i + 1) * P]
                    act.activation(row, row, ACT.Exp, bias=negmax[:, i % SLOTS, h:h + 1],
                                   accum_out=total[:, i % LSLOTS, h:h + 1]).then_inc(exp_done, 1)

                def copy_transposes(i, c):
                    act.wait_ge(turned[0], it * NC + BEFORE[i] + c + 1)
                    a, z = c * PC, min(i + 1, (c + 1) * PC)
                    act.activation(probsT[:, i % 2, 0, a:z, :],
                                   psum[4][:, 0:(z - a) * P].rearrange("p (k q) -> p k q", q=P),
                                   ACT.Copy).then_inc(copied[0], 1)

                act.wait_ge(w_in, it * (12 * 16) + 12 * 16)
                for kind in "qk":
                    for c in range(2):
                        n = place[(kind, c)]
                        act.wait_ge(filled, it * ITEMS + n + 1)
                        for half in range(2):
                            t = slice((2 * half + c) * CH, (2 * half + c + 1) * CH)
                            for h in range(2):
                                own, other = (slice(j * E, (j + 1) * E) for j in (h, 1 - h))
                                hi, bias = (k_parts, bk) if kind == "k" else (q_hi, bq)
                                for to in (own,) if kind == "k" else (own, other):
                                    last = act.activation(hi[to, h, t], psum[2 * (n % 2) + half][own, :],
                                                          ACT.Identity, bias=bias[own, 0:1])
                            last.then_inc(hi_done, 1)
                for h in range(2):
                    exponentials(0, h)
                for i in range(KT + 2):
                    for c in range(KT // PC):
                        if i < KT and c < CHUNKS[i]:
                            copy_transposes(i, c)
                        if c == 0 and i >= 2:
                            act.wait_ge(weighed, it * KT + i - 1)
                            act.activation(oT[:, i % 2, :], psum[6 + i % 2][:, 0:P], ACT.Copy).then_inc(oT_copied, 1)
                        if c < 2 and i + 1 < KT:
                            exponentials(i + 1, c)


def stage_experts(nc, f_p, f_c, f_w1, f_b1, f_w2, f_b2, f_g1, f_g1b, f_g2, f_g2b,
                  h_all, ident, banks, psum, out):
    ZPART, WPART = (0, 0, 1), (0, 1, 0)
    ZR = len(ZPART) * R
    KR = ZR + 2
    HALF = 64
    TOP = TOPK + M
    BIG = 3.0e38
    TAKEN = -3.0e38
    NSTEP = 2 * NJ
    WBANKS = 2
    SIDE = 6
    Y = 7
    PREP_ITEMS, OUT_ITEMS = 11, 3
    UNIT_ITEMS = PREP_ITEMS + OUT_ITEMS
    PREP_STEPS = 11
    EARLY = 5
    with ExitStack() as own:
        def sb(name, shape, dt=F32):
            return own.enter_context(nc.sbuf_tensor(name, shape, dt))

        def sem(name):
            return own.enter_context(nc.semaphore(name))

        z_dram = nc.dram_tensor("z_scratch", (2, P, GTOK), F32, kind="Internal").ap()

        UNITS = M * HID
        w1c = sb("w1c", [P, NQ, UNITS + M], F32R)
        w1, cm = w1c[:, :, 0:UNITS], w1c[:, :, UNITS:UNITS + M]
        w2 = sb("w2", [P, S, NJ, 2 * R])
        b2 = sb("b2", [P, 3, S, 2 * R], BF16)
        pm_hi, pm_lo = sb("pm_hi", [P, S * R]), sb("pm_lo", [DLO, S * R])
        g1, g1b, g2 = sb("g1", [P, GH]), sb("g1b", [GH, 1]), sb("g2", [GH, D])
        g2b_bc = sb("g2b_bc", [P, D])
        ident16 = sb("ident16", [P, P], F16)
        select = sb("select", [P, NJ, P], F16)
        zst = sb("zst", [P, 2, NQ, GTOK], F32R)
        rows_loaded, loaded, cleared, split, placed = sem("rows_loaded"), sem("loaded"), sem("cleared"), sem("split"), sem("placed")
        selected = sem("selected")
        N_ROWS, N_LOADS = 2 * S + 1, 2 * S + 9
        step = sem("route_step")
        pool_step = sem("pool_step")
        mean_ready, sq_ready, var_ready = sem("mean_ready"), sem("sq_ready"), sem("var_ready")
        pow_done, rstd_ready, xn_ready = sem("pow_done"), sem("rstd_ready"), sem("xn2_ready")
        side_full, side_free = sem("side_full"), sem("side_free")
        zh_done, z_split, z_stored, z_in = sem("zh_done"), sem("z_split"), sem("z_stored"), sem("z_in")
        sc_copied, den_asked, exp_asked, exp_done = (sem("sc_copied"), sem("den_asked"), sem("exp_asked2"),
                                                     sem("exp_done2"))
        marked, w_ready, w_copied, w_scaled = sem("marked"), sem("w_ready"), sem("w_copied"), sem("w_scaled")
        up_done, gelu_done = sem("up_done"), sem("gelu_done")
        spread, mixed, down_done = sem("spread"), sem("mixed"), sem("down_done")
        comb_ready, gh_ready = sem("comb_ready"), sem("gh_ready")
        out_ready, out_stored = sem("out_ready"), sem("out_stored")

        with ExitStack() as setup:
            raw1 = setup.enter_context(nc.sbuf_tensor("raw1", [P, UNITS + M], F32))
            raw1p = setup.enter_context(nc.sbuf_tensor("raw1p", [P, 2, UNITS + M], F32R))
            rawb = setup.enter_context(nc.sbuf_tensor("rawb", [S, M * HID], F32))
            rawbp = setup.enter_context(nc.sbuf_tensor("rawbp", [S, 2, M * HID], F32R))
            rawb2 = setup.enter_context(nc.sbuf_tensor("rawb2", [P, S, 2 * R], F32))
            rawb2r = setup.enter_context(nc.sbuf_tensor("rawb2r", [P, S, 2 * R], F32))
            block = setup.enter_context(nc.Block())

            def place_parts(eng, half):
                eng.wait_ge(split, 2)
                for s in range(half * NQ, (half + 1) * NQ):
                    rows = slice(s * R, (s + 1) * R)
                    q, base = s % NQ, HALF * half
                    for g, part in enumerate(WPART):
                        to = slice(base + g * R, base + (g + 1) * R)
                        eng.dma_start(w1c[to, q, :].bitcast(F32), raw1p[rows, part, :].bitcast(F32)).then_inc(placed, 16)
                    for g in range(2):
                        to = base + ZR + g
                        eng.dma_start(w1[to:to + 1, q, :].bitcast(F32), rawbp[s:s + 1, g, :].bitcast(F32))\
                           .then_inc(placed, 16)
                eng.wait_ge(placed, 16 * 5 * S)

            @block.gpsimd
            def _(pool):
                pool.memset(select[:, :, :], 0.0).then_inc(selected, 1)
                pool.memset(w2[:, :, :, :], 0.0).then_inc(cleared, 1)
                pool.memset(rawb2[:, :, :], 0.0).then_inc(cleared, 1)
                pool.tensor_copy(ident16[:, :], ident[:, :])
                for half in range(2):
                    view = select[:, :, :].rearrange("p j (e u) -> p j e u", u=HID)
                    pool.wait_ge(selected, half + 1)
                    pool.affine_select(out=view, in_=view, compare_op=ALU.not_equal, fill=1.0, base=-M * half,
                                       pattern=[[-4, NJ], [-1, 4], [0, HID]], channel_multiplier=1)\
                        .then_inc(selected, 1)

            @block.sync
            def _(sp):
                with nc.allow_non_contiguous_dma(reason="weights, once"):
                    for s in range(S):
                        rows = slice(s * R, (s + 1) * R)
                        sp.dma_start(raw1[rows, 0:UNITS].rearrange("r (m h) -> r m h", h=HID),
                                     f_w1[s].rearrange("m r h -> r m h")).then_inc(rows_loaded, 16)
                        sp.dma_start(raw1[rows, UNITS:UNITS + M], f_c[s].rearrange("m r -> r m"))\
                          .then_inc(rows_loaded, 16)
                    sp.dma_start(rawb[:, :], f_b1.rearrange("s m h -> s (m h)")).then_inc(rows_loaded, 16)
                    sp.wait_ge(cleared, 2)
                    for half in range(2):
                        for part in range(2):
                            sp.dma_start(rawb2[part * M:(part + 1) * M, half * NQ:(half + 1) * NQ,
                                               half * R:(half + 1) * R],
                                         f_b2[half * NQ:(half + 1) * NQ].rearrange("s m r -> m s r")).then_inc(loaded, 16)
                    sp.dma_start(pm_hi[:, :].rearrange("d (s r) -> d s r", r=R),
                                 f_p[:, 0:P, :].rearrange("s d r -> d s r")).then_inc(loaded, 16)
                    sp.dma_start(pm_lo[:, :].rearrange("d (s r) -> d s r", r=R),
                                 f_p[:, P:D, :].rearrange("s d r -> d s r")).then_inc(loaded, 16)
                    for s in range(S):
                        half, q = divmod(s, NQ)
                        sp.dma_start(w2[:, s, :, half * R:(half + 1) * R],
                                     f_w2[s].rearrange("m h r -> (m h) r").rearrange("(j p) r -> p j r", p=P))\
                          .then_inc(loaded, 16)
                        row = 2 * R * q + R * half
                        sp.dma_start(g1[row:row + R, :], f_g1[s * R:(s + 1) * R, :]).then_inc(loaded, 16)
                    sp.dma_start(g1b[:, :], f_g1b.rearrange("(g a) -> g a", a=1)).then_inc(loaded, 16)
                    sp.dma_start(g2[:, :], f_g2).then_inc(loaded, 16)
                    sp.dma_start(g2b_bc[:, :], f_g2b.rearrange("(a d) -> a d", a=1).to_broadcast([P, D]))\
                      .then_inc(loaded, 16)
                    place_parts(sp, 0)
                    sp.wait_ge(loaded, 16 * N_LOADS)

            @block.scalar
            def _(act):
                with nc.allow_non_contiguous_dma(reason="weights, once"):
                    place_parts(act, 1)

            @block.vector
            def _(dve):
                for base in (0, HALF):
                    dve.memset(zst[base + 32:base + HALF, :, :, :].bitcast(F32), 1.0)
                dve.wait_ge(rows_loaded, 16 * N_ROWS)
                for raw, parts in ((raw1[:, :], raw1p), (rawb[:, :], rawbp)):
                    dve.tensor_copy(parts[:, 0, :], raw).then_inc(step, 1)
                dve.wait_ge(step, 2)
                for raw, parts in ((raw1[:, :], raw1p), (rawb[:, :], rawbp)):
                    dve.tensor_tensor(parts[:, 1, :], raw, parts[:, 0, :].bitcast(F32), ALU.subtract).then_inc(split, 1)
                dve.wait_ge(loaded, 16 * N_LOADS)
                n = [2]

                def link(ins):
                    n[0] += 1
                    ins.then_inc(step, 1)
                    dve.wait_ge(step, n[0])

                link(dve.tensor_copy(b2[:, 0], rawb2[:, :, :]))
                link(dve.tensor_tensor(rawb2r[:, :, :], rawb2[:, :, :], b2[:, 0], ALU.subtract))
                link(dve.tensor_copy(b2[:, 1], rawb2r[:, :, :]))
                link(dve.tensor_tensor(rawb2r[:, :, :], rawb2r[:, :, :], b2[:, 1], ALU.subtract))
                dve.tensor_copy(b2[:, 2], rawb2r[:, :, :])

        SETUP_STEPS = 7
        x2 = sb("x2", [P, GW])
        c = sb("ln_c", [P, GW])
        sq = sb("ln_sq", [P, GW])
        small = sb("ln_small", [P, 4 * GT])
        power = sb("power", [P, GT])
        o = sb("o", [P, GW])
        xt_hi, xt_lo = sb("x2t_hi", [P, GTOK]), sb("x2t_lo", [DLO, GTOK])
        zp = sb("zp", [P, 2, GTOK], F32R)
        sc = sb("sc", [P, GT * S, TOP])
        scr = sb("scr", [P, GT * S, TOP])
        top = sb("top", [P, GT * S, 8])
        holder = sb("holder", [P, 4])
        den = sb("den", [P, GT * S, TOPK])
        rden = sb("rden", [P, 2, GT * S])
        ew = sb("ew", [P, GT * S, M])
        wsp = sb("wsp", [P, GT * S, 2, M], F16)
        wT = sb("wT", [P, 2, S, GTOK], F16)
        hid = sb("hid", [P, 2, NQ, GTOK])
        hw = sb("hw", [P, 2, NQ, GTOK])
        comb = sb("comb", [P, GTOK])
        gh = sb("gh", [GH, GTOK])
        mean, var, rstd, newton = (small[:, GT * i:GT * i + GT] for i in range(4))
        tok = lambda a: a.rearrange("p (n d) -> p n d", d=D)
        wide = lambda a: a.unsqueeze(2).to_broadcast([P, GT, D])

        def need(eng, semaphore, value):
            if not (isinstance(value, int) and value <= 0):
                eng.wait_ge(semaphore, value)

        def place(g, k):
            if isinstance(g, int) and g == -1:
                return k
            if isinstance(g, int) and g == NG - 1:
                return g * UNIT_ITEMS + k
            return g * UNIT_ITEMS + PREP_ITEMS + k

        def units(eng, prologue, unit):
            prologue()
            with eng.Fori(0, NG // 2 - 1) as gg:
                unit(gg * 2, 0, False)
                unit(gg * 2 + 1, 1, False)
            unit(NG - 2, 0, False)
            unit(NG - 1, 1, True)

        block = own.enter_context(nc.Block())

        @block.sync
        def _(sp):
            sp.sem_inc(out_stored, 16)

            def bounce_z(g, u):
                sp.wait_ge(z_split, g + 1)
                sp.dma_start(z_dram.rearrange("a p n -> p a n"), zp[:, :, :].bitcast(F32)).then_inc(z_stored, 16)
                sp.wait_ge(z_stored, g * 16 + 16)
                for base, s0 in ((0, 0), (HALF, NQ)):
                    for k, part in enumerate(ZPART):
                        sp.dma_start(zst[base + k * R:base + (k + 1) * R, u, :, :].bitcast(F32),
                                     z_dram[part, s0 * R:(s0 + NQ) * R, :].rearrange("(s r) n -> r s n", r=R))\
                          .then_inc(z_in, 16)

            def unit(g, u, final):
                if not final:
                    bounce_z(g + 1, 1 - u)
                sp.wait_ge(out_ready, g + 1)
                sp.dma_start(out[bass.ds(g * GTOK, GTOK), :].rearrange("(c p) d -> p c d", p=P), tok(o[:, :]))\
                  .then_inc(out_stored, 16)

            units(sp, lambda: bounce_z(0, 0), unit)
            sp.wait_ge(out_stored, NG * 16 + 16)

        @block.gpsimd
        def _(pool):
            pool.memset(power[:, :], -0.5)

            def centre(g):
                pool.wait_ge(mean_ready, g + 1)
                pool.tensor_tensor(tok(c[:, :]), tok(x2[:, :]), wide(mean), ALU.subtract).then_inc(pool_step, 1)
                pool.wait_ge(pool_step, g + 1)
                pool.tensor_tensor(sq[:, :], c[:, :], c[:, :], ALU.mult).then_inc(sq_ready, 1)

            def root(g):
                pool.wait_ge(var_ready, g + 1)
                pool.tensor_tensor(rstd, var, power[:, :], ALU.pow).then_inc(pow_done, 1)

            def scale(g):
                pool.wait_ge(rstd_ready, g + 1)
                pool.tensor_tensor(tok(x2[:, :]), tok(c[:, :]), wide(rstd), ALU.mult).then_inc(xn_ready, 1)

            def below_best(g):
                pool.wait_ge(den_asked, g + 1)
                pool.tensor_tensor(ew[:, :, :], sc[:, :, 0:M],
                                   top[:, :, TOPK:TOPK + 1].to_broadcast([P, GT * S, M]), ALU.subtract)\
                    .then_inc(exp_asked, 1)

            def divide(g):
                pool.wait_ge(marked, g + 1)
                pool.tensor_tensor(ew[:, :, :], ew[:, :, :],
                                   rden[:, 1, :].unsqueeze(2).to_broadcast([P, GT * S, M]), ALU.mult)\
                    .then_inc(w_scaled, 1)

            def prepare(g):
                centre(g)
                root(g)
                scale(g)
                below_best(g)
                divide(g)

            units(pool, lambda: prepare(0), lambda g, u, final: None if final else prepare(g + 1))

        @block.tensor
        def _(pe):
            def side(g, item):
                need(pe, side_free, place(g, item))

            def turn_x(g, part):
                side(g - 1, part)
                if part == 0:
                    pe.wait_ge(xn_ready, g + 1)
                d0 = (0, DLO)[part]
                for t in range(GT):
                    last = pe.transpose(psum[SIDE][:, t * P:(t + 1) * P], x2[:, t * D + d0:t * D + d0 + P],
                                        ident[:, :])
                last.then_inc(side_full, 1)

            def make_z(g):
                side(g - 1, 2)
                pe.matmul(psum[SIDE], pm_hi[:, :], xt_hi[:, :], start=True, stop=False)
                pe.matmul(psum[SIDE], pm_lo[:, :], xt_lo[:, :], start=False, stop=True).then_inc(side_full, 1)

            def score(g, u, k):
                side(g - 1, 3 + k)
                if k == 0:
                    pe.wait_ge(z_in, g * 96 + 96)
                half, t2 = divmod(k, 2)
                rows = slice(HALF * half, HALF * half + ZR)
                for t in (2 * t2, 2 * t2 + 1):
                    for q in range(NQ):
                        at = ((t % 2) * NQ + q) * M
                        last = pe.matmul(psum[SIDE][:, at:at + M], zst[rows, u, q, t * P:(t + 1) * P],
                                         cm[rows, q, :], start=True, stop=True)
                last.then_inc(side_full, 1)

            def turn_w(g, k):
                side(g - 1, 7 + k)
                if k == 0:
                    pe.wait_ge(w_ready, g + 1)
                dst = psum[SIDE].bitcast(F16)
                for s in (2 * k, 2 * k + 1):
                    for t in range(GT):
                        at = (s % 2) * GTOK + t * P
                        last = pe.transpose(dst[:, at:at + P], wsp[:, t * S + s, :, :].rearrange("p a m -> p (a m)"),
                                            ident16[:, :])
                last.then_inc(side_full, 1)

            def up(g, u, n):
                half, j = divmod(n, NJ)
                need(pe, gelu_done, g * (2 * NSTEP) + 2 * n)
                rows = slice(HALF * half, HALF * half + KR)
                for q in range(NQ):
                    last = pe.matmul(psum[q], w1[rows, q, j * P:(j + 1) * P], zst[rows, u, q, :],
                                     start=True, stop=True)
                    if q % 2:
                        last.then_inc(up_done, 1)

            def spread_weights(g, u, n, qs):
                half, j = divmod(n, NJ)
                for q in qs:
                    need(pe, mixed, g * (NQ * NSTEP) + NQ * n + q - WBANKS + 1)
                    pe.matmul(psum[4 + q % WBANKS], select[:, j, :], wT[:, u, q + NQ * half, :],
                              start=True, stop=True).then_inc(spread, 1)

            def down(g, n):
                for q in range(NQ):
                    if q < 2:
                        pe.wait_ge(mixed, g * (NQ * NSTEP) + NQ * n + (1, NQ)[q])
                    last = pe.matmul(psum[Y][32 * q:32 * q + 32, :], w2[:, q + NQ * (n // NJ), n % NJ, :],
                                     hw[:, n % 2, q, :], start=False, stop=(n == NSTEP - 1))
                last.then_inc(down_done, 1)

            def bias_down(g, u):
                need(pe, comb_ready, g)
                for s in range(S):
                    q, half = s % NQ, s // NQ
                    for part in range(3):
                        pe.matmul(psum[Y][32 * q:32 * q + 32, :], b2[:, part, s, :], wT[:, u, s, :],
                                  start=(half == 0 and part == 0), stop=False)

            def mixture_up(g):
                side(g, PREP_ITEMS)
                pe.wait_ge(comb_ready, g + 1)
                pe.matmul(psum[SIDE][0:GH, :], g1[:, :], comb[:, :], start=True, stop=True).then_inc(side_full, 1)

            def mixture_down(g, k):
                side(g, PREP_ITEMS + 1 + k)
                for t in (2 * k, 2 * k + 1):
                    last = pe.matmul(psum[SIDE][:, (t % 2) * 256:(t % 2) * 256 + D], gh[:, t * P:(t + 1) * P],
                                     g2[:, :], start=True, stop=True)
                last.then_inc(side_full, 1)

            def one_step(g, u, n, preparing, last_group):
                h, v = g + 1, 1 - u
                if preparing:
                    if n in (9, 10):
                        turn_x(h, n - 9)
                    if n == 11:
                        make_z(h)
                    if 13 <= n < 17:
                        score(h, v, n - 13)
                    if 26 <= n < 30:
                        turn_w(h, n - 26)
                spread_weights(g, u, n, (0, 1))
                if n == 1:
                    bias_down(g, u)
                if n:
                    down(g, n - 1)
                elif not (isinstance(g, int) and g == 0):
                    down(g - 1, NSTEP - 1)
                spread_weights(g, u, n, (2, 3))
                if n < NSTEP - 1:
                    up(g, u, n + 1)
                elif not last_group:
                    up(h, v, 0)

            def prologue():
                for part in range(2):
                    turn_x(0, part)
                make_z(0)
                for k in range(4):
                    score(0, 0, k)
                for k in range(4):
                    turn_w(0, k)
                pe.wait_ge(w_copied, 4)
                up(0, 0, 0)
                for n in range(EARLY):
                    one_step(0, 0, n, False, False)

            def unit(g, u, final):
                for n in range(EARLY, NSTEP):
                    one_step(g, u, n, not final, final)
                if final:
                    down(g, NSTEP - 1)
                    mixture_up(g)
                    for k in range(2):
                        mixture_down(g, k)
                else:
                    pe.wait_ge(w_copied, g * 4 + 8)
                    for n in range(EARLY):
                        one_step(g + 1, 1 - u, n, False, False)
                        if n == 2:
                            mixture_up(g)
                        if n > 2:
                            mixture_down(g, n - 3)

            units(pe, prologue, unit)

        @block.scalar
        def _(act):
            def item(g, k):
                act.wait_ge(side_full, place(g, k) + 1)

            def take_x(g, part):
                item(g - 1, part)
                act.activation((xt_hi, xt_lo)[part][:, :], psum[SIDE][(0, P - DLO)[part]:P, :], ACT.Copy)\
                   .then_inc(side_free, 1)

            def take_z(g):
                item(g - 1, 2)
                act.activation(zp[:, 0, :], psum[SIDE], ACT.Copy).then_inc(zh_done, 1)

            def take_scores(g, k):
                item(g - 1, 3 + k)
                half, t2 = divmod(k, 2)
                act.activation(sc[:, :, :].rearrange("p (t s) m -> p t s m", s=S)
                               [:, 2 * t2:2 * t2 + 2, half * NQ:(half + 1) * NQ, 0:M],
                               psum[SIDE].rearrange("p (t q m) -> p t q m", t=2, m=M), ACT.Copy)\
                   .then_inc(side_free, 1)

            def exponentials(g):
                act.wait_ge(exp_asked, g + 1)
                act.activation(den[:, :, :], den[:, :, :], ACT.Exp)
                act.activation(ew[:, :, :], ew[:, :, :], ACT.Exp).then_inc(exp_done, 1)

            def take_w(g, u, k):
                item(g - 1, 7 + k)
                act.activation(wT[:, u, 2 * k:2 * k + 2, :], psum[SIDE].bitcast(F16)
                               .rearrange("p (s n) -> p s n", n=GTOK), ACT.Copy).then_inc(w_copied, 1)
                act.wait_ge(w_copied, g * 4 + k + 1)
                act.sem_inc(side_free, 1)

            def gelus(g, n):
                need(act, mixed, g * (NQ * NSTEP) + NQ * (n - 1))
                for pair in range(2):
                    act.wait_ge(up_done, g * (2 * NSTEP) + 2 * n + pair + 1)
                    act.activation(hid[:, n % 2, 2 * pair:2 * pair + 2, :],
                                   banks[:, pair * 1024:(pair + 1) * 1024].rearrange("p (q n) -> p q n", n=GTOK),
                                   ACT.Gelu_apprx_tanh).then_inc(gelu_done, 1)

            def mixture_gelu(g):
                item(g, PREP_ITEMS)
                act.activation(gh[:, :], psum[SIDE][0:GH, :], ACT.Gelu_apprx_tanh, bias=g1b[:, 0:1])\
                   .then_inc(side_free, 1)

            def one_step(g, u, n, preparing):
                gelus(g, n)
                if preparing:
                    h, v = g + 1, 1 - u
                    if n in (9, 10):
                        take_x(h, n - 9)
                    if n == 11:
                        take_z(h)
                    if 13 <= n < 17:
                        take_scores(h, n - 13)
                    if n == 20:
                        exponentials(h)
                    if 26 <= n < 30:
                        take_w(h, v, n - 26)

            def prologue():
                for part in range(2):
                    take_x(0, part)
                take_z(0)
                for k in range(4):
                    take_scores(0, k)
                exponentials(0)
                for k in range(4):
                    take_w(0, 0, k)
                for n in range(EARLY):
                    one_step(0, 0, n, False)

            def unit(g, u, final):
                for n in range(EARLY, NSTEP):
                    one_step(g, u, n, not final)
                if final:
                    mixture_gelu(g)
                else:
                    for n in range(EARLY):
                        one_step(g + 1, 1 - u, n, False)
                        if n == 2:
                            mixture_gelu(g)

            units(act, prologue, unit)

        @block.vector
        def _(dve):
            dve.memset(sc[:, :, M:TOP], BIG).then_inc(step, 1)
            dve.wait_ge(step, SETUP_STEPS)
            steps = [0]

            def link(g, ins):
                steps[0] += 1
                ins.then_inc(step, 1)
                dve.wait_ge(step, g * PREP_STEPS + (steps[0] - 1) % PREP_STEPS + 1 + SETUP_STEPS)

            def sums(g):
                link(g, dve.tensor_scalar(x2[:, :], h_all[:, bass.ds(g * GW, GW)], 1.0, None, ALU.mult))
                link(g, dve.tensor_reduce(mean, tok(x2[:, :]), AX.X, ALU.add))
                dve.tensor_scalar(mean, mean, 1.0 / D, None, ALU.mult).then_inc(mean_ready, 1)

            def variance(g):
                dve.wait_ge(sq_ready, g + 1)
                link(g, dve.tensor_reduce(var, tok(sq[:, :]), AX.X, ALU.add))
                dve.tensor_scalar(var, var, 1.0 / D, LNEPS, ALU.mult, ALU.add).then_inc(var_ready, 1)

            def refine(g):
                dve.wait_ge(pow_done, g + 1)
                link(g, dve.tensor_tensor(newton, rstd, rstd, ALU.mult))
                link(g, dve.tensor_tensor(newton, newton, var, ALU.mult))
                link(g, dve.tensor_scalar(newton, newton, -0.5, 1.5, ALU.mult, ALU.add))
                dve.tensor_tensor(rstd, rstd, newton, ALU.mult).then_inc(rstd_ready, 1)

            def split_z(g):
                dve.wait_ge(zh_done, g + 1)
                dve.tensor_tensor(zp[:, 1, :], psum[SIDE], zp[:, 0, :].bitcast(F32), ALU.subtract)\
                   .then_inc(z_split, 1)
                dve.wait_ge(z_split, g + 1)
                dve.sem_inc(side_free, 1)

            def top_four(g, k):
                half, t2 = divmod(k, 2)
                dve.wait_ge(side_free, place(g - 1, 3 + k) + 1)
                dve.memset(holder[:, k:k + 1], 0.0)
                for t in (2 * t2, 2 * t2 + 1):
                    for q in range(NQ):
                        i = t * S + half * NQ + q
                        last = dve.max(top[:, i, :], sc[:, i, :])
                if k == 3:
                    link(g, last)

            def denominators(g):
                dve.tensor_tensor(den[:, :, :], top[:, :, TOPK:2 * TOPK],
                                  top[:, :, TOPK:TOPK + 1].to_broadcast([P, GT * S, TOPK]), ALU.subtract)\
                   .then_inc(den_asked, 1)

            def mark(g, part):
                for i in range(part * GT * S // 2, (part + 1) * GT * S // 2):
                    last = dve.match_replace(scr[:, i, :], top[:, i, :], sc[:, i, :], TAKEN)
                if part:
                    link(g, last)

            def reciprocals(g):
                dve.wait_ge(exp_done, g + 1)
                link(g, dve.tensor_reduce(rden[:, 0, :], den[:, :, :], AX.X, ALU.add))
                link(g, dve.reciprocal(rden[:, 1, :], rden[:, 0, :]))

            def keep_marked(g):
                dve.scalar_tensor_tensor(ew[:, :, :], scr[:, :, 0:M], TAKEN, ew[:, :, :], ALU.is_equal, ALU.mult)\
                   .then_inc(marked, 1)

            def split_weights(g):
                dve.wait_ge(w_scaled, g + 1)
                link(g, dve.tensor_copy(wsp[:, :, 0, :], ew[:, :, :]))
                dve.tensor_tensor(wsp[:, :, 1, :], ew[:, :, :], wsp[:, :, 0, :], ALU.subtract).then_inc(w_ready, 1)

            def mix(g, n):
                need(dve, down_done, g * NSTEP + n - 1)
                for q in range(NQ):
                    dve.wait_ge(gelu_done, g * (2 * NSTEP) + 2 * n + q // 2 + 1)
                    dve.wait_ge(spread, g * (NQ * NSTEP) + NQ * n + q + 1)
                    dve.tensor_tensor(hw[:, n % 2, q, :], hid[:, n % 2, q, :], psum[4 + q % WBANKS],
                                      ALU.mult).then_inc(mixed, 1)

            def take_mixture(g):
                dve.wait_ge(down_done, g * NSTEP + NSTEP)
                dve.tensor_copy(comb[:, :], psum[Y]).then_inc(comb_ready, 1)

            def take_out(g, k):
                if k == 0:
                    dve.wait_ge(out_stored, g * 16 + 16)
                dve.wait_ge(side_full, place(g, PREP_ITEMS + 1 + k) + 1)
                dve.tensor_tensor(tok(o[:, :])[:, 2 * k:2 * k + 2, :],
                                  psum[SIDE].rearrange("p (t n) -> p t n", t=2)[:, :, 0:D],
                                  g2b_bc[:, :].unsqueeze(1).to_broadcast([P, 2, D]), ALU.add).then_inc(side_free, 1)
                if k:
                    dve.wait_ge(side_free, place(g, UNIT_ITEMS))
                    dve.tensor_tensor(o[:, :], o[:, :], h_all[:, bass.ds(g * GW, GW)], ALU.add)\
                       .then_inc(out_ready, 1)

            def one_step(g, n, preparing):
                mix(g, n)
                if preparing:
                    h = g + 1
                    if n == 5:
                        sums(h)
                    if n == 7:
                        variance(h)
                    if n == 8:
                        refine(h)
                    if n == 11:
                        split_z(h)
                    if 14 <= n < 18:
                        top_four(h, n - 14)
                    if n == 18:
                        denominators(h)
                    if n in (18, 19):
                        mark(h, n - 18)
                    if n == 21:
                        reciprocals(h)
                        keep_marked(h)
                    if n == 24:
                        split_weights(h)

            def prologue():
                sums(0)
                variance(0)
                refine(0)
                split_z(0)
                for k in range(4):
                    top_four(0, k)
                denominators(0)
                for part in range(2):
                    mark(0, part)
                reciprocals(0)
                keep_marked(0)
                split_weights(0)
                assert steps[0] == PREP_STEPS, steps
                for n in range(EARLY):
                    one_step(0, n, False)

            def unit(g, u, final):
                for n in range(EARLY, NSTEP):
                    one_step(g, n, not final)
                if final:
                    take_mixture(g)
                    take_out(g, 0)
                    take_out(g, 1)
                else:
                    for n in range(EARLY):
                        one_step(g + 1, n, False)
                        if n == 0:
                            take_mixture(g)
                        if n > 2:
                            take_out(g, n - 3)

            units(dve, prologue, unit)


_INS = ['x', 'L0_tok_weight', 'L0_attn_W_Q', 'L0_attn_b_Q', 'L0_attn_W_K', 'L0_attn_b_K', 'L0_attn_W_V',
        'L0_attn_b_V', 'L0_attn_W_O', 'L0_attn_b_O', 'L0_ffn_P', 'L0_ffn_C', 'L0_ffn_W1', 'L0_ffn_b1',
        'L0_ffn_W2', 'L0_ffn_b2', 'L0_ffn_G1', 'L0_ffn_g1b', 'L0_ffn_G2', 'L0_ffn_g2b']
STAGES = 3


def kernel(**inputs):
    import numpy as np
    import concourse.bacc as bacc
    from concourse.bass_utils import run_bass_kernel_spmd

    nc = bacc.Bacc("TRN2", target_bir_lowering=False, num_devices=1)
    arrays, args = {}, []
    for name in _INS:
        a = np.ascontiguousarray(inputs[name])
        if name == 'x':
            a = np.ascontiguousarray(a.reshape(NT, P).T)
        arrays[f"in_{name}"] = a
        args.append(nc.dram_tensor(f"in_{name}", a.shape, mybir.dt.from_np(a.dtype), kind="ExternalInput").ap())
    o = nc.dram_tensor("out_h", (B * T, D), F32, kind="ExternalOutput").ap()
    tower(nc, *args, o, stages=STAGES)
    r = run_bass_kernel_spmd(nc, [arrays], core_ids=[0])
    return r.results[0]["out_h"].reshape(B, T, D)
```
